# Optimizing a Trainium2 kernel written in Bass

```python
import numpy as np
import jax
import jax.numpy as jnp

def _softmax(x, axis=-1):
    return jax.nn.softmax(x, axis=axis)

def _gelu(x):
    return jax.nn.gelu(x, approximate=True)

def _silu(x):
    return jax.nn.silu(x)

def _sigmoid(x):
    return jax.nn.sigmoid(x)

def _layernorm(x, axis=-1, eps=1e-05):
    m = jnp.mean(x, axis=axis, keepdims=True)
    v = jnp.var(x, axis=axis, keepdims=True)
    return (x - m) / jnp.sqrt(v + eps)

def _scatter_add(tgt, idx, src, axis=0):
    return tgt.at[idx].add(src)

def _segment_sum(src, seg, n):
    return jax.ops.segment_sum(src, seg, n)
kernel_name = 'mk_seq_postln_d1_jaxref_r8_c66989'

def setup_inputs(seed: int=0):
    np.random.seed(seed)
    _w = jnp.asarray

    def _L0_attn_setup():
        import jax, jax.numpy as jnp
        import numpy as np
        D_MODEL = 128
        N_HEADS = 16
        D_HEAD = D_MODEL // N_HEADS
        M_SLOPE = 0.5
        BATCH = 2
        SEQ = 256

        def _alibi_bias(n_heads, seq_len, m, dtype):
            slopes = m ** jnp.arange(n_heads, dtype=dtype)
            pos = jnp.arange(seq_len, dtype=dtype)
            dist = jnp.abs(pos[:, None] - pos[None, :])
            return -dist[None, :, :] * slopes[:, None, None]
        key = jax.random.key(seed)
        k1, k2, k3 = jax.random.split(key, 3)
        x = jax.random.normal(k1, (BATCH, SEQ, D_MODEL), dtype=jnp.float32)
        qkv_w = jax.random.normal(k2, (3 * D_MODEL, D_MODEL), dtype=jnp.float32) * (1.0 / np.sqrt(D_MODEL))
        qkv_b = jnp.zeros((3 * D_MODEL,), dtype=jnp.float32)
        out_w = jax.random.normal(k3, (D_MODEL, D_MODEL), dtype=jnp.float32) * (1.0 / np.sqrt(D_MODEL))
        out_b = jnp.zeros((D_MODEL,), dtype=jnp.float32)
        return {'x': x, 'qkv_w': qkv_w, 'qkv_b': qkv_b, 'out_w': out_w, 'out_b': out_b}
    _L0_attn_in = _L0_attn_setup()

    def _L0_ffn_setup():
        import jax, jax.numpy as jnp
        import numpy as np
        S_LEN, BATCH, HIDDEN = (256, 2, 128)
        N_HEADS, N_KV = (16, 8)
        N_EXP, TOP_K, CAP_F = (8, 2, 1.25)
        FFN = 512
        HEAD_DIM = HIDDEN // N_HEADS
        Q_PER_KV = N_HEADS // N_KV
        EPS = 1e-05
        NEG = -1000000000.0

        def _ln(x, w, b):
            mu = jnp.mean(x, -1, keepdims=True)
            var = jnp.var(x, -1, keepdims=True)
            return (x - mu) * jax.lax.rsqrt(var + EPS) * w + b

        def _forward(hidden_states, ln1_weight, ln1_bias, ln2_weight, ln2_bias, qkv_weight, proj_weight, router_weight, moe_w1, moe_w2):
            S, B, H = hidden_states.shape
            ln1 = _ln(hidden_states, ln1_weight, ln1_bias)
            qkv = (ln1 @ qkv_weight.T).reshape(S, B, N_KV, (Q_PER_KV + 2) * HEAD_DIM)
            q_dim = Q_PER_KV * HEAD_DIM
            q = qkv[..., :q_dim].reshape(S, B, N_HEADS, HEAD_DIM)
            k = jnp.repeat(qkv[..., q_dim:q_dim + HEAD_DIM], Q_PER_KV, axis=2)
            v = jnp.repeat(qkv[..., q_dim + HEAD_DIM:], Q_PER_KV, axis=2)
            scores = jnp.einsum('sbhd,tbhd->bhst', q, k) / jnp.sqrt(jnp.float32(HEAD_DIM))
            causal = jnp.tril(jnp.ones((S, S), bool))
            attn = jax.nn.softmax(jnp.where(causal[None, None], scores, NEG), axis=-1)
            attn_out = jnp.einsum('bhst,tbhd->sbhd', attn, v).reshape(S, B, H)
            hidden_after_attn = hidden_states + attn_out @ proj_weight.T
            x = _ln(hidden_after_attn, ln2_weight, ln2_bias).reshape(-1, H)
            N = S * B
            probs = jax.nn.softmax(x.astype(jnp.float32) @ router_weight, axis=-1)
            top_p, top_i = jax.lax.top_k(probs, TOP_K)
            top_p = top_p / jnp.sum(top_p, -1, keepdims=True)
            flat_exp = top_i.reshape(-1)
            order = jnp.argsort(flat_exp)
            sorted_exp = flat_exp[order]
            counts = jnp.bincount(sorted_exp, length=N_EXP)
            offsets = jnp.concatenate([jnp.zeros((1,), counts.dtype), jnp.cumsum(counts)])
            within = jnp.arange(N * TOP_K) - offsets[sorted_exp]
            cap = int(np.ceil(N * TOP_K / N_EXP * CAP_F))
            keep = within < cap
            slot = jnp.where(keep, sorted_exp * cap + within, N_EXP * cap)
            tok_id = order // TOP_K
            padded_tokens = jnp.zeros((N_EXP * cap + 1, H), x.dtype).at[slot].set(x[tok_id])[:-1]
            padded_probs = jnp.zeros((N_EXP * cap + 1,), jnp.float32).at[slot].set(top_p.reshape(-1)[order])[:-1]
            padded_ids = jnp.zeros((N_EXP * cap + 1,), jnp.int32).at[slot].set(tok_id.astype(jnp.int32))[:-1]
            exp_in = padded_tokens.reshape(N_EXP, cap, H)
            act = jax.nn.gelu(jnp.einsum('ech,ehf->ecf', exp_in, moe_w1), approximate=False)
            exp_out = jnp.einsum('ecf,efh->ech', act, moe_w2).reshape(N_EXP * cap, H)
            weighted = exp_out * padded_probs[:, None].astype(exp_out.dtype)
            moe = jnp.zeros((N, H), exp_out.dtype).at[padded_ids].add(weighted)
            return hidden_after_attn + moe.reshape(S, B, H)
        ks = jax.random.split(jax.random.key(seed), 6)
        qkv_out = N_KV * (Q_PER_KV + 2) * HEAD_DIM
        sc = 0.02
        return {'hidden_states': jax.random.normal(ks[0], (S_LEN, BATCH, HIDDEN), jnp.float32), 'ln1_weight': jnp.ones((HIDDEN,), jnp.float32), 'ln1_bias': jnp.zeros((HIDDEN,), jnp.float32), 'ln2_weight': jnp.ones((HIDDEN,), jnp.float32), 'ln2_bias': jnp.zeros((HIDDEN,), jnp.float32), 'qkv_weight': jax.random.normal(ks[1], (qkv_out, HIDDEN), jnp.float32) * sc, 'proj_weight': jax.random.normal(ks[2], (HIDDEN, HIDDEN), jnp.float32) * sc, 'router_weight': jax.random.normal(ks[3], (HIDDEN, N_EXP), jnp.float32) * sc, 'moe_w1': jax.random.normal(ks[4], (N_EXP, HIDDEN, FFN), jnp.float32) * sc, 'moe_w2': jax.random.normal(ks[5], (N_EXP, FFN, HIDDEN), jnp.float32) * sc}
    _L0_ffn_in = _L0_ffn_setup()
    _d = {'L0_attn_x': _L0_attn_in['x'], 'L0_attn_qkv_w': _L0_attn_in['qkv_w'], 'L0_attn_qkv_b': _L0_attn_in['qkv_b'], 'L0_attn_out_w': _L0_attn_in['out_w'], 'L0_attn_out_b': _L0_attn_in['out_b'], 'L0_ffn_ln1_weight': _L0_ffn_in['ln1_weight'], 'L0_ffn_ln1_bias': _L0_ffn_in['ln1_bias'], 'L0_ffn_ln2_weight': _L0_ffn_in['ln2_weight'], 'L0_ffn_ln2_bias': _L0_ffn_in['ln2_bias'], 'L0_ffn_qkv_weight': _L0_ffn_in['qkv_weight'], 'L0_ffn_proj_weight': _L0_ffn_in['proj_weight'], 'L0_ffn_router_weight': _L0_ffn_in['router_weight'], 'L0_ffn_moe_w1': _L0_ffn_in['moe_w1'], 'L0_ffn_moe_w2': _L0_ffn_in['moe_w2']}
    _x0 = _d['L0_attn_x']
    _d['L0_attn_x'] = jax.random.normal(jax.random.fold_in(jax.random.key(seed), 1), (2, 1024, 128), dtype=_x0.dtype)
    del _x0
    return _d

def reference(L0_attn_x, L0_attn_qkv_w, L0_attn_qkv_b, L0_attn_out_w, L0_attn_out_b, L0_ffn_ln1_weight, L0_ffn_ln1_bias, L0_ffn_ln2_weight, L0_ffn_ln2_bias, L0_ffn_qkv_weight, L0_ffn_proj_weight, L0_ffn_router_weight, L0_ffn_moe_w1, L0_ffn_moe_w2):

    def _L0_attn_ref(x, qkv_w, qkv_b, out_w, out_b):
        import jax, jax.numpy as jnp
        import numpy as np
        D_MODEL = 128
        N_HEADS = 16
        D_HEAD = D_MODEL // N_HEADS
        M_SLOPE = 0.5
        BATCH = 2
        SEQ = 256

        def _alibi_bias(n_heads, seq_len, m, dtype):
            slopes = m ** jnp.arange(n_heads, dtype=dtype)
            pos = jnp.arange(seq_len, dtype=dtype)
            dist = jnp.abs(pos[:, None] - pos[None, :])
            return -dist[None, :, :] * slopes[:, None, None]
        batch, seq_len, d_model = x.shape
        qkv = x @ qkv_w.T + qkv_b
        qkv = qkv.reshape(batch, seq_len, N_HEADS, 3 * D_HEAD).transpose(0, 2, 1, 3)
        q, k, v = jnp.split(qkv, 3, axis=-1)
        scale = jnp.sqrt(jnp.asarray(D_HEAD, dtype=x.dtype))
        scores = jnp.einsum('bhid,bhjd->bhij', q, k) / scale
        scores = scores + _alibi_bias(N_HEADS, seq_len, M_SLOPE, x.dtype)[None]
        attn = jax.nn.softmax(scores, axis=-1)
        out = jnp.einsum('bhij,bhjd->bhid', attn, v)
        out = out.transpose(0, 2, 1, 3).reshape(batch, seq_len, d_model)
        return out @ out_w.T + out_b

    def _L0_ffn_ref(hidden_states, ln1_weight, ln1_bias, ln2_weight, ln2_bias, qkv_weight, proj_weight, router_weight, moe_w1, moe_w2):
        import jax, jax.numpy as jnp
        import numpy as np
        S_LEN, BATCH, HIDDEN = (256, 2, 128)
        N_HEADS, N_KV = (16, 8)
        N_EXP, TOP_K, CAP_F = (8, 2, 1.25)
        FFN = 512
        HEAD_DIM = HIDDEN // N_HEADS
        Q_PER_KV = N_HEADS // N_KV
        EPS = 1e-05
        NEG = -1000000000.0

        def _ln(x, w, b):
            mu = jnp.mean(x, -1, keepdims=True)
            var = jnp.var(x, -1, keepdims=True)
            return (x - mu) * jax.lax.rsqrt(var + EPS) * w + b

        def _forward(hidden_states, ln1_weight, ln1_bias, ln2_weight, ln2_bias, qkv_weight, proj_weight, router_weight, moe_w1, moe_w2):
            S, B, H = hidden_states.shape
            ln1 = _ln(hidden_states, ln1_weight, ln1_bias)
            qkv = (ln1 @ qkv_weight.T).reshape(S, B, N_KV, (Q_PER_KV + 2) * HEAD_DIM)
            q_dim = Q_PER_KV * HEAD_DIM
            q = qkv[..., :q_dim].reshape(S, B, N_HEADS, HEAD_DIM)
            k = jnp.repeat(qkv[..., q_dim:q_dim + HEAD_DIM], Q_PER_KV, axis=2)
            v = jnp.repeat(qkv[..., q_dim + HEAD_DIM:], Q_PER_KV, axis=2)
            scores = jnp.einsum('sbhd,tbhd->bhst', q, k) / jnp.sqrt(jnp.float32(HEAD_DIM))
            causal = jnp.tril(jnp.ones((S, S), bool))
            attn = jax.nn.softmax(jnp.where(causal[None, None], scores, NEG), axis=-1)
            attn_out = jnp.einsum('bhst,tbhd->sbhd', attn, v).reshape(S, B, H)
            hidden_after_attn = hidden_states + attn_out @ proj_weight.T
            x = _ln(hidden_after_attn, ln2_weight, ln2_bias).reshape(-1, H)
            N = S * B
            probs = jax.nn.softmax(x.astype(jnp.float32) @ router_weight, axis=-1)
            top_p, top_i = jax.lax.top_k(probs, TOP_K)
            top_p = top_p / jnp.sum(top_p, -1, keepdims=True)
            flat_exp = top_i.reshape(-1)
            order = jnp.argsort(flat_exp)
            sorted_exp = flat_exp[order]
            counts = jnp.bincount(sorted_exp, length=N_EXP)
            offsets = jnp.concatenate([jnp.zeros((1,), counts.dtype), jnp.cumsum(counts)])
            within = jnp.arange(N * TOP_K) - offsets[sorted_exp]
            cap = int(np.ceil(N * TOP_K / N_EXP * CAP_F))
            keep = within < cap
            slot = jnp.where(keep, sorted_exp * cap + within, N_EXP * cap)
            tok_id = order // TOP_K
            padded_tokens = jnp.zeros((N_EXP * cap + 1, H), x.dtype).at[slot].set(x[tok_id])[:-1]
            padded_probs = jnp.zeros((N_EXP * cap + 1,), jnp.float32).at[slot].set(top_p.reshape(-1)[order])[:-1]
            padded_ids = jnp.zeros((N_EXP * cap + 1,), jnp.int32).at[slot].set(tok_id.astype(jnp.int32))[:-1]
            exp_in = padded_tokens.reshape(N_EXP, cap, H)
            act = jax.nn.gelu(jnp.einsum('ech,ehf->ecf', exp_in, moe_w1), approximate=False)
            exp_out = jnp.einsum('ecf,efh->ech', act, moe_w2).reshape(N_EXP * cap, H)
            weighted = exp_out * padded_probs[:, None].astype(exp_out.dtype)
            moe = jnp.zeros((N, H), exp_out.dtype).at[padded_ids].add(weighted)
            return hidden_after_attn + moe.reshape(S, B, H)
        return _forward(hidden_states, ln1_weight, ln1_bias, ln2_weight, ln2_bias, qkv_weight, proj_weight, router_weight, moe_w1, moe_w2)
    x = L0_attn_x
    x = _layernorm(x + _L0_attn_ref(x, L0_attn_qkv_w, L0_attn_qkv_b, L0_attn_out_w, L0_attn_out_b), axis=-1)
    x = _layernorm(x + _L0_ffn_ref(x, L0_ffn_ln1_weight, L0_ffn_ln1_bias, L0_ffn_ln2_weight, L0_ffn_ln2_bias, L0_ffn_qkv_weight, L0_ffn_proj_weight, L0_ffn_router_weight, L0_ffn_moe_w1, L0_ffn_moe_w2), axis=-1)
    return x

_drawn_inputs = setup_inputs


def setup_inputs(seed=0):
    import zlib

    import numpy as np

    out = dict(_drawn_inputs(seed))
    spreads = {'L0_attn_qkv_b': (0.0, 0.1),
     'L0_attn_out_b': (0.0, 0.1),
     'L0_ffn_ln1_weight': (1.0, 0.6),
     'L0_ffn_ln1_bias': (0.0, 0.8),
     'L0_ffn_ln2_weight': (1.0, 0.6),
     'L0_ffn_ln2_bias': (0.0, 0.8)}
    factors = {'L0_ffn_router_weight': 3.366, 'L0_ffn_moe_w1': 2.905, 'L0_ffn_moe_w2': 2.873}
    for name, (base, spread) in spreads.items():
        noise = np.random.default_rng([zlib.crc32(name.encode()), seed]).standard_normal(out[name].shape)
        drawn = base * np.exp(spread * noise) if base else spread * noise
        out[name] = jnp.asarray(drawn.astype(out[name].dtype))
    for name, factor in factors.items():
        out[name] = (out[name] * factor).astype(out[name].dtype)
    return out
```

```python
from contextlib import ExitStack

import concourse.bass as bass
from concourse import mybir

F32 = mybir.dt.float32
BF16 = mybir.dt.bfloat16
U32 = mybir.dt.uint32
I32 = mybir.dt.int32
ALU = mybir.AluOpType
ACT = mybir.ActivationFunctionType
AX = mybir.AxisListType

P = 128
S = 2
N = 1024
D = 128
H = 16
DH = D // H
NB = N // P
NT = S * NB
UNITS = S * H
HALF = N // 2
QUARTER = N // 4
LAG = 2
SCALE = float(DH) ** -0.5

PARTS = 3
PRODUCTS = PARTS * PARTS * DH
ROW_ALIBI = PRODUCTS
ROW_MAX = ROW_ALIBI + 3 * NB
K_MAX = ROW_MAX
K_EXP = ROW_MAX + PARTS
SLOTS = 4
LOADS = 4


def attention_and_prep(nc, t, keep):
    with ExitStack() as ctx:
        def sb(name, shape, dt=F32):
            return ctx.enter_context(nc.sbuf_tensor(name, shape, dt))

        def sem(name):
            return ctx.enter_context(nc.semaphore(name))

        ps = ctx.enter_context(nc.psum_tensor("ps", [P, 8, 512], F32))

        x_tok, ident, head_out = keep["x_tok"], keep["ident"], keep["head_out"]
        w_nat = sb("w_nat", [P, 3, D])
        w_t = sb("w_t", [D, 3, D])
        x_t = sb("x_t", [D, S * N])
        bias_qk = sb("bias_qk", [P, 2])
        bias_q_scaled = sb("bias_q_scaled", [P, 1])
        bias_v = sb("bias_v", [P, H, DH])
        proj = sb("proj", [P, 2, 512])
        rest = sb("rest", [P, 2, 512])
        parts = sb("parts", [P, 2, PARTS, 512], BF16)
        v_all = sb("v_all", [P, UNITS, NB, DH + 1])
        q_stack = [sb(f"q_stack{k}", [K_EXP, N], BF16) for k in range(SLOTS)]
        k_stack = [sb(f"k_stack{k}", [K_EXP, N], BF16) for k in range(SLOTS)]
        slope_eye = [sb(f"slope_eye{k}", [P, P], BF16) for k in range(SLOTS)]
        v_unit = [sb(f"v_unit{k}", [P, NB, 32]) for k in range(SLOTS)]
        distance = sb("distance", [P, P], BF16)
        pick = sb("pick", [P, 64])
        max_half = sb("max_half", [P, 2, NB, 2])
        row_max = sb("row_max", [P, 2, NB])
        max_t = sb("max_t", [NB, 2, P])
        max_rest = sb("max_rest", [NB, 2, P])
        max_parts = sb("max_parts", [NB, 2, PARTS, P], BF16)
        no_bits = sb("no_bits", [NB, P])
        probs = sb("probs", [P, 4, N])
        out_t = sb("out_t", [P, QUARTER])
        recip = sb("recip", [P, 2, 4])

        ps_s = [ps[:, 0:2, :], ps[:, 2:4, :]]
        ps_m = [ps[:, 4, :], ps[:, 5, :]]
        ps_o = ps[:, 6, 0:QUARTER]
        ps_c = ps[:, 7, :]

        ld_w, ld_x, ld_bias, ld_const = sem("ld_w"), sem("ld_x"), sem("ld_bias"), sem("ld_const")
        w_turned, w_kept = sem("w_turned"), sem("w_kept")
        x_turned, x_kept = sem("x_turned"), sem("x_kept")
        bq_ready = sem("bq_ready")
        qk_ready, qf_ready, q1_ready, r1_ready, q2_ready, q3_ready = (
            sem("qk_ready"), sem("qf_ready"), sem("q1_ready"), sem("r1_ready"), sem("q2_ready"), sem("q3_ready"))
        parts_saved = [sem(f"parts_saved{b}") for b in range(2)]
        v_ready, v_kept, v_ones = sem("v_ready"), sem("v_kept"), sem("v_ones")
        loaded = [sem(f"loaded{k}") for k in range(SLOTS)]
        max_loaded = [sem(f"max_loaded{k}") for k in range(SLOTS)]
        max_saved = sem("max_saved")
        v_copied = sem("v_copied")
        mx_full, mx_used = sem("mx_full"), sem("mx_used")
        max_done, maxt_full, maxt_kept, split, max_split = (
            sem("max_done"), sem("maxt_full"), sem("maxt_kept"), sem("split"), sem("max_split"))
        s_full, p_ready, pv_done = sem("s_full"), sem("p_ready"), sem("pv_done")
        o_kept, tok_full, recip_done, tok_kept = sem("o_kept"), sem("tok_full"), sem("recip_done"), sem("tok_kept")

        qk_dram = t["qk_dram"]
        max_dram = t["max_dram"]

        TURNS = (UNITS - 4) // SLOTS

        def each_unit(eng, body, lead=2):
            for m in range(lead):
                body(m, m)
            with eng.Fori(0, TURNS) as turn:
                for k in range(lead, lead + SLOTS):
                    body(turn * SLOTS + k, k % SLOTS)
            for m in range(lead + SLOTS * TURNS, UNITS):
                body(m, m % SLOTS)

        def known(m):
            return m if isinstance(m, int) else None

        def first(m):
            return known(m) == 0

        def has_next(m, ahead):
            return known(m) is None or m + ahead < UNITS

        def turn_of(m, slot):
            return (m - slot) // SLOTS + 1

        block = ctx.enter_context(nc.Block())

        @block.sync
        def _(sp):
            sp.dma_start(w_nat[:], t["qkv_w"].rearrange("(a p) d -> p a d", p=P)).then_inc(ld_w, 16)
            sp.dma_start(ident[:], t["c_ident"]).then_inc(ld_w, 16)
            for s in range(S):
                sp.dma_start(x_tok[:, s * NB:(s + 1) * NB, :],
                             t["x"][s].rearrange("(a p) d -> p a d", p=P)).then_inc(ld_x, 16)
            with nc.allow_non_contiguous_dma(reason="bias per output row"):
                b = t["qkv_b"].rearrange("(h c d) -> c h d", h=H, c=3)
                for c in range(2):
                    for h in range(H):
                        sp.dma_start(bias_qk[h * DH:(h + 1) * DH, c:c + 1],
                                     b[c, h].rearrange("(d o) -> d o", o=1)).then_inc(ld_bias, 16)
            sp.dma_start(bias_v[:], b[2].partition_broadcast(P)).then_inc(ld_bias, 16)
            sp.dma_start(distance[:], t["c_distance"]).then_inc(ld_const, 16)
            for k in range(SLOTS):
                sp.dma_start(q_stack[k][ROW_ALIBI:ROW_MAX, :], t["c_alibi_q"]).then_inc(ld_const, 16)
                sp.dma_start(k_stack[k][ROW_MAX:K_EXP, :], t["c_minus"]).then_inc(ld_const, 16)
            sp.dma_start(pick[:], t["c_pick"]).then_inc(ld_const, 16)

            for y in range(8):
                s, c, half = y // 4, (y // 2) % 2, y % 2
                sp.wait_ge(q3_ready, y + 1)
                for a in range(PARTS):
                    dst = qk_dram[c, s * H:(s + 1) * H, :, :, :, half * 512:(half + 1) * 512]
                    dst = dst[:, :, a] if c == 0 else dst[:, a]
                    for r in range(PARTS):
                        sp.dma_start(dst[:, r], parts[:, y % 2, a, :]).then_inc(parts_saved[y % 2], 16)

            def load(m, slot):
                unit = bass.ds(m, 1)
                for c, stack in ((0, q_stack), (1, k_stack)):
                    sp.dma_start(stack[slot][0:PRODUCTS, :],
                                 qk_dram[c, unit].rearrange("o a b d n -> (o a b d) n")).then_inc(loaded[slot], 16)
                sp.dma_start(k_stack[slot][ROW_ALIBI:ROW_MAX, :],
                             t["c_alibi_k"][unit].rearrange("o p n -> (o p) n")).then_inc(loaded[slot], 16)
                sp.dma_start(slope_eye[slot][:],
                             t["c_slope_eye"][unit].rearrange("o p c -> (o p) c")).then_inc(loaded[slot], 16)

            def load_max(m, slot):
                sp.wait_ge(max_split, m + 1)
                b = slot % 2
                sp.dma_start(max_dram[b].rearrange("a (i c) -> i a c", c=P),
                             max_parts[:, b, :, :]).then_inc(max_saved, 16)
                sp.wait_ge(max_saved, 16 * m + 16)
                sp.dma_start(q_stack[slot][ROW_MAX:K_EXP, :], max_dram[b]).then_inc(max_loaded[slot], 16)

            for b in range(2):
                sp.wait_ge(parts_saved[b], 16 * 4 * PARTS * PARTS)
            for m in range(3):
                load(m, m)
            load_max(0, 0)

            def body(m, slot):
                if not first(m):
                    sp.wait_ge(s_full, m * NB)
                if has_next(m, 3):
                    load(m + 3, (slot + 3) % 4)
                if has_next(m, 1):
                    load_max(m + 1, (slot + 1) % 4)

            each_unit(sp, body, lead=1)

        @block.gpsimd
        def _(pool):
            pool.memset(v_all[:], 1.0).then_inc(v_ones, 1)
            for k in range(SLOTS):
                pool.memset(v_unit[k][:], 0.0).then_inc(v_ones, 1)
            pool.memset(no_bits[:], 0.0).then_inc(v_ones, 1)
            pool.wait_ge(v_ones, 2 + SLOTS)

            def copy_v(m, slot):
                pool.tensor_copy(v_unit[slot][:, :, 0:DH + 1],
                                 v_all[:, bass.ds(m, 1), :, :].rearrange("p o a c -> p (o a) c")).then_inc(v_copied, 1)

            def split_max(m, slot):
                b = slot % 2
                src, rst, out = max_t[:, b, :], max_rest[:, b, :], max_parts[:, b, :, :]
                pool.wait_ge(maxt_kept, m + 1)
                if not (isinstance(m, int) and m < 2):
                    pool.wait_ge(max_saved, 16 * m - 16)
                pool.tensor_tensor(out[:, 0, :], src, no_bits[:], ALU.add).then_inc(split, 1)
                pool.wait_ge(split, 3 * m + 1)
                pool.tensor_tensor(rst, src, out[:, 0, :], ALU.subtract).then_inc(split, 1)
                pool.wait_ge(split, 3 * m + 2)
                pool.tensor_tensor(out[:, 1, :], rst, no_bits[:], ALU.add).then_inc(split, 1)
                pool.wait_ge(split, 3 * m + 3)
                pool.tensor_tensor(out[:, 2, :], rst, out[:, 1, :], ALU.subtract).then_inc(max_split, 1)

            pool.wait_ge(v_kept, NT // 4)
            copy_v(0, 0)
            copy_v(1, 1)
            split_max(0, 0)

            def body(m, slot):
                if has_next(m, 2) and not (known(m) is not None and m < 2):
                    pool.wait_ge(pv_done, NB * m - NB)
                if has_next(m, 1):
                    split_max(m + 1, (slot + 1) % 4)
                if has_next(m, 2):
                    copy_v(m + 2, (slot + 2) % 4)

            each_unit(pool, body)

        @block.tensor
        def _(pe):
            pe.wait_ge(ld_w, 32)
            for a in range(3):
                mm = pe.transpose(ps[:, 0, a * P:(a + 1) * P], w_nat[:, a, :], ident[:])
            mm.then_inc(w_turned, 1)
            for g in range(4):
                pe.wait_ge(ld_x, 32)
                for j in range(4):
                    mm = pe.transpose(ps[:, 1 + g, j * P:(j + 1) * P], x_tok[:, 4 * g + j, :], ident[:])
                mm.then_inc(x_turned, 1)
            pe.wait_ge(w_kept, 3)
            for y in range(8):
                s, c, half = y // 4, (y // 2) % 2, y % 2
                g = s * 2 + half
                pe.wait_ge(x_kept, g + 1)
                if y >= 3:
                    pe.wait_ge(qf_ready, y - 2)
                pe.matmul(ps[:, 5 + y % 3, :], w_t[:, c, :], x_t[:, g * 512:(g + 1) * 512],
                          start=True, stop=True).then_inc(qk_ready, 1)
                if y % 2 == 1:
                    gv = y // 2
                    pe.wait_ge(x_kept, gv + 1)
                    for j in range(4):
                        tile = 4 * gv + j
                        mm = pe.matmul(ps[:, 1 + gv, j * P:(j + 1) * P], x_t[:, tile * P:(tile + 1) * P],
                                       w_t[:, 2, :], start=True, stop=True)
                    mm.then_inc(v_ready, 1)

            def scores(out, rows, stack, rhs, slot, block, h):
                on_diagonal = block // 4 == h
                mm = pe.matmul(out, stack[slot][0:rows, block * P:(block + 1) * P],
                               rhs[slot][0:rows, HALF * h:HALF * (h + 1)], start=True, stop=not on_diagonal)
                if on_diagonal:
                    a = P * (block % 4)
                    mm = pe.matmul(out[:, a:a + P], slope_eye[slot][:], distance[:], start=False, stop=True)
                return mm

            def max_bank(m, slot, i, h):
                if not (isinstance(m, int) and m == 0 and i == 0):
                    pe.wait_ge(mx_used, 16 * m + (2 * i + h - 1))
                scores(ps_m[h], K_MAX, q_stack, k_stack, slot, i, h).then_inc(mx_full, 1)

            def exp_bank(slot, j, h, which):
                return scores(ps_s[which][:, h, :], K_EXP, k_stack, q_stack, slot, j, h)

            def turn_max(m, slot):
                pe.wait_ge(max_done, m + 1)
                if not (isinstance(m, int) and m < 1):
                    pe.wait_ge(maxt_kept, m)
                pe.transpose(ps_c[0:NB, P:2 * P], row_max[:, slot % 2, :], ident[:]).then_inc(maxt_full, 1)

            def values(m, slot, j):
                pe.wait_ge(p_ready, m * NB + (j + 1))
                if j == 0:
                    pe.wait_ge(v_copied, m + 1)
                    if not first(m):
                        pe.wait_ge(o_kept, m)
                for c in range(4):
                    mm = pe.matmul(ps_o[32 * c:32 * c + 32, :], v_unit[slot][:, j, :],
                                   probs[:, j % 4, QUARTER * c:QUARTER * (c + 1)],
                                   start=(j == 0), stop=(j == NB - 1), tile_position=(0, 32 * c))
                mm.then_inc(pv_done, 1)

            def to_tokens(m):
                pe.wait_ge(o_kept, m + 1)
                for b in range(2):
                    mm = pe.matmul(ps_c[:, 64 * b:64 * b + 64], out_t[:, b * P:(b + 1) * P], pick[:],
                                   start=True, stop=True)
                mm.then_inc(tok_full, 1)

            pe.wait_ge(ld_const, 16 * 10)
            pe.wait_ge(qf_ready, 8)
            pe.wait_ge(v_kept, 4)
            for m in range(2):
                pe.wait_ge(loaded[m], 16 * LOADS)
                for i in range(NB):
                    for h in range(2):
                        max_bank(m, m, i, h)
                if m == 0:
                    turn_max(0, 0)

            def body(m, slot):
                nxt = (slot + 2) % 4
                for j in range(NB):
                    if j == 0:
                        pe.wait_ge(max_loaded[slot], turn_of(m, slot) * 16)
                        if has_next(m, 2):
                            pe.wait_ge(loaded[nxt], turn_of(m + 2, nxt) * (16 * LOADS))
                    if not (first(m) and j < 2):
                        pe.wait_ge(p_ready, m * NB + (j - 1))
                    if has_next(m, 2):
                        max_bank(m + 2, nxt, j, 0)
                    for h in range(2):
                        mm = exp_bank(slot, j, h, j % 2)
                    mm.then_inc(s_full, 1)
                    if has_next(m, 2):
                        max_bank(m + 2, nxt, j, 1)
                    if j >= LAG:
                        values(m, slot, j - LAG)
                    elif not first(m):
                        values(m - 1, (slot - 1) % 4, NB - LAG + j)
                    if j == 1 and has_next(m, 1):
                        if not (known(m) is not None and m < 2):
                            pe.wait_ge(tok_kept, m - 1)
                        turn_max(m + 1, (slot + 1) % 4)
                    if j == 4 and not first(m):
                        if has_next(m, 1):
                            pe.wait_ge(maxt_kept, m + 2)
                        else:
                            pe.wait_ge(tok_kept, m - 1)
                        to_tokens(m - 1)

            each_unit(pe, body)
            for j in range(NB - LAG, NB):
                values(UNITS - 1, (UNITS - 1) % 4, j)
            pe.wait_ge(tok_kept, UNITS - 1)
            to_tokens(UNITS - 1)

        @block.scalar
        def _(act):
            for g in range(0, 4, 2):
                act.wait_ge(x_turned, g + 2)
                act.copy(x_t[:, g * 512:(g + 1) * 512], ps[:, 1 + g, :]).then_inc(x_kept, 1)
                act.copy(x_t[:, (g + 1) * 512:(g + 2) * 512], ps[:, 2 + g, :]).then_inc(x_kept, 1)
            act.wait_ge(bq_ready, 1)
            act.wait_ge(ld_bias, 16 * 33)
            for y in range(8):
                c = (y // 2) % 2
                b = y % 2
                act.wait_ge(qk_ready, y + 1)
                if y >= 2:
                    act.wait_ge(r1_ready, y - 1)
                act.activation(proj[:, b, :], ps[:, 5 + y % 3, :], ACT.Identity,
                               bias=(bias_q_scaled[:, 0:1] if c == 0 else bias_qk[:, 1:2]),
                               scale=(SCALE if c == 0 else 1.0)).then_inc(qf_ready, 1)
                act.wait_ge(qf_ready, y + 1)
                if y >= 2:
                    act.wait_ge(parts_saved[b], 16 * PARTS * PARTS * (y // 2))
                act.copy(parts[:, b, 0, :], proj[:, b, :]).then_inc(q1_ready, 1)
                act.wait_ge(r1_ready, y + 1)
                act.copy(parts[:, b, 1, :], rest[:, b, :]).then_inc(q2_ready, 1)

            def keep_max(m, slot):
                act.wait_ge(maxt_full, m + 1)
                if not (isinstance(m, int) and m < 2):
                    act.wait_ge(max_split, m - 1)
                act.copy(max_t[:, slot % 2, :], ps_c[0:NB, P:2 * P]).then_inc(maxt_kept, 1)

            def keep_out(m):
                act.wait_ge(pv_done, NB * m + NB)
                if not first(m):
                    act.wait_ge(tok_full, m)
                act.copy(out_t[:], ps_o).then_inc(o_kept, 1)

            keep_max(0, 0)

            def body(m, slot):
                for j in range(NB):
                    act.wait_ge(s_full, m * NB + (j + 1))
                    if not (first(m) and j < 4):
                        act.wait_ge(pv_done, NB * m + (j - 3))
                    act.activation(probs[:, j % 4, :], ps_s[j % 2].rearrange("p a n -> p (a n)"),
                                   ACT.Exp).then_inc(p_ready, 1)
                    if j == 1 and not first(m):
                        keep_out(m - 1)
                    if j == 2 and has_next(m, 1):
                        keep_max(m + 1, (slot + 1) % 4)

            each_unit(act, body)
            keep_out(UNITS - 1)

        @block.vector
        def _(dve):
            dve.wait_ge(ld_bias, 16 * 33)
            dve.tensor_scalar(bias_q_scaled[:], bias_qk[:, 0:1], SCALE, None, ALU.mult).then_inc(bq_ready, 1)
            dve.wait_ge(w_turned, 1)
            for c in range(3):
                dve.tensor_copy(w_t[:, c, :].rearrange("p (h d) -> p h d", h=H),
                                ps[:, 0, 0:3 * D].rearrange("p (h c d) -> p c h d", h=H, c=3)[:, c]
                                ).then_inc(w_kept, 1)
            dve.wait_ge(v_ones, 1)
            for y in range(8):
                b = y % 2
                dve.wait_ge(q1_ready, y + 1)
                if y >= 2:
                    dve.wait_ge(q3_ready, y - 1)
                dve.tensor_tensor(rest[:, b, :], proj[:, b, :], parts[:, b, 0, :], ALU.subtract).then_inc(r1_ready, 1)
                dve.wait_ge(q2_ready, y + 1)
                dve.wait_ge(r1_ready, y + 1)
                dve.tensor_tensor(parts[:, b, 2, :], rest[:, b, :], parts[:, b, 1, :],
                                  ALU.subtract).then_inc(q3_ready, 1)
                if y % 2 == 1:
                    gv = y // 2
                    s, blk = gv // 2, 4 * (gv % 2)
                    dve.wait_ge(v_ready, gv + 1)
                    for a in range(4):
                        last = dve.tensor_tensor(
                            v_all[:, s * H:(s + 1) * H, blk + a, 0:DH],
                            ps[:, 1 + gv, a * P:(a + 1) * P].rearrange("p (h d) -> p h d", h=H),
                            bias_v[:], ALU.add)
                    last.then_inc(v_kept, 1)

            def reduce_bank(m, slot, g):
                dve.wait_ge(mx_full, 16 * m + (g + 1))
                dve.tensor_reduce(max_half[:, slot % 2, g // 2, g % 2:g % 2 + 1], ps_m[g % 2],
                                  AX.X, ALU.max).then_inc(mx_used, 1)

            def join_max(m, slot):
                dve.wait_ge(mx_used, 16 * m + 16)
                if not (isinstance(m, int) and m < 2):
                    dve.wait_ge(maxt_full, m - 1)
                dve.tensor_reduce(row_max[:, slot % 2, :], max_half[:, slot % 2, :, :], AX.X,
                                  ALU.max).then_inc(max_done, 1)

            def keep_tokens(m):
                v = ps_c[:, 0:P].rearrange("p (b c r) -> p b c r", b=2, c=4)
                dve.wait_ge(tok_full, m + 1)
                if not first(m):
                    dve.wait_ge(tok_kept, m)
                dve.reciprocal(recip[:], v[:, :, :, DH]).then_inc(recip_done, 1)
                dve.wait_ge(recip_done, m + 1)
                out = head_out[:, :, bass.ds(m, 1), :].rearrange("p (c b) o d -> p b c (o d)", b=2)
                dve.tensor_tensor(out, v[:, :, :, 0:DH], recip[:].unsqueeze(3).broadcast_to([P, 2, 4, DH]),
                                  ALU.mult).then_inc(tok_kept, 1)

            for m in range(2):
                for g in range(16):
                    reduce_bank(m, m, g)
                join_max(m, m)

            def body(m, slot):
                if has_next(m, 2):
                    dve.wait_ge(max_done, m + 1)
                for g in range(16):
                    if has_next(m, 2):
                        reduce_bank(m + 2, (slot + 2) % 4, g)
                    if g == 11 and not first(m):
                        keep_tokens(m - 1)
                if has_next(m, 2):
                    join_max(m + 2, (slot + 2) % 4)

            each_unit(dve, body)
            keep_tokens(UNITS - 1)


EXPERTS = 8
TOP = 2
CAP = 640
CT = CAP // P
F = 512
FT = F // P
KV = 8
QKV = 256
CHUNKS = 4
BC = NB // CHUNKS
TC = S * BC
EPS = 1e-5


def second_half(nc, t, keep):
    with ExitStack() as ctx:
        def sb(name, shape, dt=F32):
            return ctx.enter_context(nc.sbuf_tensor(name, shape, dt))

        def sem(name):
            return ctx.enter_context(nc.semaphore(name))

        ps = ctx.enter_context(nc.psum_tensor("ps2", [P, 8, 512], F32))
        x_tok, ident, head_out = keep["x_tok"], keep["ident"], keep["head_out"]

        wo_nat, wq_nat, wp_nat = sb("wo_nat", [P, D]), sb("wq_nat", [P, 2, D]), sb("wp_nat", [P, D])
        wo_t, wq_t, wp_t = sb("wo_t", [D, D]), sb("wq_t", [D, QKV]), sb("wp_t", [D, D])
        router = sb("router", [D, EXPERTS])
        rows = {n: sb(f"row_{n}", [P, D]) for n in ("out_b", "ln1_w", "ln1_b", "ln2_w", "ln2_b")}
        before = sb("before", [P, P], BF16)
        ones = sb("ones", [P, P], BF16)
        expert_rank = sb("expert_rank", [P, NT * EXPERTS])
        expert_base = sb("expert_base", [P, NT * EXPERTS])
        eps = sb("eps", [P, 1])
        zeros = sb("zeros", [P, CT * D])
        turned = sb("turned", [P, CHUNKS, TC, P])
        x1 = sb("x1", [P, NT, D])
        l1 = sb("l1", [P, NT, D])
        qkv = sb("qkv", [P, NT, QKV])
        att = sb("att", [P, NT, D])
        hid = sb("hid", [P, NT, D])
        x2 = sb("x2", [P, NT, D])
        base = sb("base", [P, NT, D])
        stats = sb("stats", [P, NT, 6])
        mv = [sb(f"mv{i}", [P, NT, 2]) for i in range(3)]
        std = [sb(f"std{i}", [P, NT]) for i in range(3)]
        rstd = [sb(f"rstd{i}", [P, NT]) for i in range(3)]
        prod = sb("prod", [P, 2, 2, D])
        mix = sb("mix", [P, 2, 2, D])
        sc = sb("sc", [P, NB, 2, H])
        sc_max = sb("sc_max", [P, NB, H])
        sc_e = sb("sc_e", [P, NB, 2, H])
        sc_sum = sb("sc_sum", [P, NB, H])
        sc_p = sb("sc_p", [P, NB, 2, H])
        logit = sb("logit", [P, NT, EXPERTS])
        lmax = sb("lmax", [P, NT])
        lexp = sb("lexp", [P, NT, EXPERTS])
        lsum = sb("lsum", [P, NT])
        lprob = sb("lprob", [P, NT, EXPERTS])
        rest = sb("rest2", [P, NT, EXPERTS])
        cand = sb("cand", [P, NT, EXPERTS])
        best = sb("best", [P, NT])
        top = [sb(f"top{k}", [P, NT]) for k in range(TOP)]
        hot = [sb(f"hot{k}", [P, NT, EXPERTS]) for k in range(TOP)]
        hot_any = sb("hot_any", [P, NT, EXPERTS], BF16)
        fits = sb("fits", [P, NT, EXPERTS])
        slot_of = sb("slot_of", [P, NT, EXPERTS])
        slot_f = sb("slot_f", [P, TOP, NT])
        slot_u = sb("slot_u", [P, TOP, NT], U32)
        top_sum = sb("top_sum", [P, NT])
        weight = [sb(f"weight{k}", [P, NT]) for k in range(TOP)]

        ld_w, ld_rows, ld_const = sem("ld_w2"), sem("ld_rows"), sem("ld_const2")
        xd_zeroed = sem("xd_zeroed")
        set_up = sem("set_up")
        wo_turned, w_kept = sem("wo_turned"), sem("w_kept2")
        chain = sem("chain")
        o_turned, o_kept = sem("o_turned"), sem("o_kept2")
        a_ready, a_summed = sem("a_ready"), sem("a_summed")
        var_ready, std_ready = [sem(f"var_ready{i}") for i in range(4)], [sem(f"std_ready{i}") for i in range(3)]
        x1_ready, l1_ready = sem("x1_ready"), sem("l1_ready")
        l_turned, l_kept = sem("l_turned"), sem("l_kept")
        qkv_ready, qkv_kept = sem("qkv_ready2"), sem("qkv_kept")
        sc_ready, sc_exp, att1_ready, att0_ready = sem("sc_ready"), sem("sc_exp"), sem("att1_ready"), sem("att0_ready")
        att_turned, att_kept = sem("att_turned"), sem("att_kept")
        p_ready, hid_ready, base_ready = sem("proj_ready"), sem("hid_ready"), sem("base_ready")
        x2_ready = sem("x2_ready")
        x2_turned, x2_kept = sem("x2_turned"), sem("x2_kept")
        logit_ready, logit_less_max, exp_ready = sem("logit_ready"), sem("logit_less_max"), sem("exp_ready")
        hot_ready, rank_ready, slots_ready = sem("hot_ready"), sem("rank_ready"), sem("slots_ready")
        scattered = sem("scattered")

        xd, yd = t["xd"], t["yd"]
        keep.update(base=base, slot_u=slot_u, weight=weight, eps=eps, scattered=scattered)
        route = ctx.enter_context(ExitStack())
        block = route.enter_context(nc.Block())

        def tiles(a, c):
            return a[:].rearrange("p (s b) d -> p s b d", s=S)[:, :, c * BC:(c + 1) * BC, :]

        def tiles3(a, c):
            return a[:].rearrange("p (s b) -> p s b", s=S)[:, :, c * BC:(c + 1) * BC]

        def tile_of(c, j):
            return (j // BC) * NB + c * BC + j % BC

        @block.sync
        def _(sp):
            sp.dma_start(wo_nat[:], t["out_w"]).then_inc(ld_w, 16)
            sp.dma_start(wq_nat[:], t["qkv_w2"].rearrange("(a p) d -> p a d", p=P)).then_inc(ld_w, 16)
            sp.dma_start(wp_nat[:], t["proj_w"]).then_inc(ld_w, 16)
            sp.dma_start(router[:], t["router"]).then_inc(ld_w, 16)
            for n, a in rows.items():
                sp.dma_start(a[:], t[n].partition_broadcast(P)).then_inc(ld_rows, 16)
            sp.dma_start(before[:], t["c_before"]).then_inc(ld_const, 16)
            sp.dma_start(expert_rank[:], t["c_experts"][0].partition_broadcast(P)).then_inc(ld_const, 16)
            sp.dma_start(expert_base[:], t["c_experts"][1].partition_broadcast(P)).then_inc(ld_const, 16)
            sp.wait_ge(set_up, 3)
            for e in range(EXPERTS):
                sp.dma_start(xd[e * CAP:(e + 1) * CAP, :].rearrange("(p a) d -> p (a d)", p=P),
                             zeros[:]).then_inc(xd_zeroed, 16)
            sp.dma_start(yd[EXPERTS * CAP:EXPERTS * CAP + 1, :], zeros[0:1, 0:D]).then_inc(xd_zeroed, 16)

        @block.gpsimd
        def _(pool):
            pool.memset(ones[:], 1.0).then_inc(set_up, 1)
            pool.memset(eps[:], EPS).then_inc(set_up, 1)
            pool.memset(zeros[:], 0.0).then_inc(set_up, 1)
            for b in range(NB):
                pool.wait_ge(qkv_kept, 2 * (b // BC) + 2)
                v0 = qkv[:, b, :].rearrange("p (g c) -> p g c", g=KV)[:, :, 24:32]
                pool.tensor_copy(att[:, b, :].rearrange("p (g r d) -> p g r d", g=KV, r=2),
                                 v0.unsqueeze(2).broadcast_to([P, KV, 2, DH])).then_inc(att0_ready, 1)
            for c in range(CHUNKS):
                pool.wait_ge(hid_ready, c + 1)
                pool.tensor_tensor(tiles(base, c), tiles(hid, c), tiles(x1, c), ALU.add).then_inc(base_ready, 1)
            pool.wait_ge(xd_zeroed, 16 * (EXPERTS + 1))
            pool.wait_ge(slots_ready, 1)
            for k in range(TOP):
                for a in range(NT):
                    pool.indirect_dma_start(
                        out=xd, out_offset=bass.IndirectOffsetOnAxis(ap=slot_u[:, k, a:a + 1], axis=0),
                        in_=x2[:, a, :], in_offset=None, bounds_check=EXPERTS * CAP - 1,
                        oob_is_err=False).then_inc(scattered, 16)
            pool.wait_ge(scattered, 16 * TOP * NT)

        @block.tensor
        def _(pe):
            pe.wait_ge(ld_w, 64)
            pe.transpose(ps[:, 7, 0:P], wo_nat[:], ident[:])
            for a in range(2):
                pe.transpose(ps[:, 7, (1 + a) * P:(2 + a) * P], wq_nat[:, a, :], ident[:])
            pe.transpose(ps[:, 7, 3 * P:4 * P], wp_nat[:], ident[:]).then_inc(wo_turned, 1)
            for c in range(CHUNKS):
                for j in range(TC):
                    a = tile_of(c, j)
                    s, b = a // NB, a % NB
                    mm = pe.transpose(ps[:, c, j * P:(j + 1) * P],
                                      head_out[:, b, s * H:(s + 1) * H, :], ident[:])
                mm.then_inc(o_turned, 1)
            pe.wait_ge(w_kept, 3)
            for c in range(CHUNKS):
                pe.wait_ge(o_kept, c + 1)
                for j in range(TC):
                    mm = pe.matmul(ps[:, 4 + c, j * P:(j + 1) * P], turned[:, c, j, :], wo_t[:],
                                   start=True, stop=True)
                mm.then_inc(a_ready, 1)
            for c in range(CHUNKS):
                pe.wait_ge(l1_ready, c + 1)
                for j in range(TC):
                    mm = pe.transpose(ps[:, c, j * P:(j + 1) * P], l1[:, tile_of(c, j), :], ident[:])
                mm.then_inc(l_turned, 1)
            for c in range(CHUNKS):
                pe.wait_ge(l_kept, 4 if c >= 2 else c + 1)
                for j in range(TC):
                    bank = (4 + 2 * c + j // 2) % 8
                    pe.wait_ge(a_summed, CHUNKS)
                    mm = pe.matmul(ps[:, bank, (j % 2) * QKV:(j % 2 + 1) * QKV], turned[:, c, j, :], wq_t[:],
                                   start=True, stop=True)
                    if j % 2 == 1:
                        mm.then_inc(qkv_ready, 1)
            for c in range(CHUNKS):
                pe.wait_ge(att0_ready, BC * (c + 1))
                pe.wait_ge(att1_ready, BC * (c + 1))
                pe.wait_ge(qkv_kept, 4)
                for j in range(TC):
                    mm = pe.transpose(ps[:, 4 + c, j * P:(j + 1) * P], att[:, tile_of(c, j), :], ident[:])
                mm.then_inc(att_turned, 1)
            pe.wait_ge(qkv_kept, 8)
            for c in range(CHUNKS):
                pe.wait_ge(att_kept, c + 1)
                for j in range(TC):
                    mm = pe.matmul(ps[:, c, j * P:(j + 1) * P], turned[:, c, j, :], wp_t[:],
                                   start=True, stop=True)
                mm.then_inc(p_ready, 1)
            for c in range(CHUNKS):
                pe.wait_ge(x2_ready, c + 1)
                for j in range(TC):
                    mm = pe.transpose(ps[:, 4 + c, j * P:(j + 1) * P], x2[:, tile_of(c, j), :], ident[:])
                mm.then_inc(x2_turned, 1)
            for c in range(CHUNKS):
                pe.wait_ge(x2_kept, c + 1)
                for j in range(TC):
                    a = tile_of(c, j)
                    mm = pe.matmul(ps[:, 0, a * EXPERTS:(a + 1) * EXPERTS], turned[:, c, j, :], router[:],
                                   start=True, stop=True)
            mm.then_inc(logit_ready, 1)
            pe.wait_ge(ld_const, 48)
            pe.wait_ge(hot_ready, 1)
            pe.matmul(ps[:, 1, 0:P], before[:], hot_any[:].rearrange("p a e -> p (a e)"), start=True, stop=False)
            for a in range(NT - 1):
                later = NT - 1 - a
                mm = pe.matmul(ps[:, 1, (a + 1) * EXPERTS:P], ones[:],
                               hot_any[:, a, :].unsqueeze(1).broadcast_to([P, later, EXPERTS]),
                               start=False, stop=(a == NT - 2))
            mm.then_inc(rank_ready, 1)

        @block.scalar
        def _(act):
            def keep_turned(ready, kept, first_bank):
                for c in range(CHUNKS):
                    act.wait_ge(ready, c + 1)
                    act.copy(turned[:, c].rearrange("p a d -> p (a d)"), ps[:, first_bank + c, :]).then_inc(kept, 1)

            def roots(i):
                for c in range(CHUNKS):
                    act.wait_ge(var_ready[i], c + 1)
                    act.activation(tiles3(std[i], c), tiles(mv[i], c)[:, :, :, 1], ACT.Sqrt,
                                   bias=eps[:, 0:1]).then_inc(std_ready[i], 1)

            act.wait_ge(set_up, 3)
            keep_turned(o_turned, o_kept, 0)
            roots(0)
            roots(1)
            act.wait_ge(a_ready, CHUNKS)
            keep_turned(l_turned, l_kept, 0)
            for c in range(CHUNKS):
                for h in range(2):
                    act.wait_ge(qkv_ready, 2 * c + h + 1)
                    act.copy(qkv[:, h * NB + c * BC:h * NB + (c + 1) * BC, :],
                             ps[:, (4 + 2 * c + h) % 8, :].rearrange("p (b n) -> p b n", b=BC)).then_inc(qkv_kept, 1)
            act.wait_ge(sc_ready, 1)
            act.activation(sc_e[:], sc[:], ACT.Exp, scale=SCALE).then_inc(sc_exp, 1)
            keep_turned(att_turned, att_kept, 4)
            roots(2)
            act.wait_ge(p_ready, CHUNKS)
            keep_turned(x2_turned, x2_kept, 4)
            act.wait_ge(logit_less_max, 1)
            act.activation(lexp[:], logit[:], ACT.Exp).then_inc(exp_ready, 1)

        @block.vector
        def _(dve):
            n = [0]

            def done(ins):
                n[0] += 1
                ins.then_inc(chain, 1)
                dve.wait_ge(chain, n[0])

            def norm_stats(i, src, c):
                for j in range(TC):
                    a = tile_of(c, j)
                    last = dve.bn_stats(stats[:, a, :], src[:, a, :])
                done(last)
                for j in range(TC):
                    a = tile_of(c, j)
                    last = dve.bn_aggr(mv[i][:, a, :], stats[:, a, :])
                last.then_inc(var_ready[i], 1)

            def inverse_std(i, c):
                dve.wait_ge(std_ready[i], c + 1)
                done(dve.reciprocal(tiles3(rstd[i], c), tiles3(std[i], c)))

            def affine_norm(i, out, src, w, b, c, ready):
                inverse_std(i, c)
                dve.wait_ge(ld_rows, 80)
                for j in range(TC):
                    a = tile_of(c, j)
                    last = dve.scalar_tensor_tensor(out=out[:, a, :], in0=src[:, a, :], scalar=mv[i][:, a, 0:1],
                                                    in1=w[:], op0=ALU.subtract, op1=ALU.mult)
                done(last)
                for j in range(TC):
                    a = tile_of(c, j)
                    last = dve.scalar_tensor_tensor(out=out[:, a, :], in0=out[:, a, :], scalar=rstd[i][:, a:a + 1],
                                                    in1=b[:], op0=ALU.mult, op1=ALU.add)
                last.then_inc(ready, 1)

            dve.wait_ge(wo_turned, 1)
            dve.tensor_copy(wo_t[:], ps[:, 7, 0:P]).then_inc(w_kept, 1)
            dve.tensor_copy(wq_t[:], ps[:, 7, P:3 * P]).then_inc(w_kept, 1)
            dve.tensor_copy(wp_t[:], ps[:, 7, 3 * P:4 * P]).then_inc(w_kept, 1)
            dve.wait_ge(ld_rows, 80)
            done(dve.tensor_tensor(x_tok[:], x_tok[:], rows["out_b"][:].unsqueeze(1).broadcast_to([P, NT, D]), ALU.add))
            for c in range(CHUNKS):
                dve.wait_ge(a_ready, c + 1)
                ins = dve.tensor_tensor(tiles(hid, c), tiles(x_tok, c),
                                        ps[:, 4 + c, :].rearrange("p (s b d) -> p s b d", s=S, b=BC), ALU.add)
                ins.then_inc(a_summed, 1)
                dve.wait_ge(a_summed, c + 1)
                norm_stats(0, hid, c)
            for c in range(CHUNKS):
                inverse_std(0, c)
                for j in range(TC):
                    a = tile_of(c, j)
                    last = dve.tensor_scalar(x1[:, a, :], hid[:, a, :], mv[0][:, a, 0:1], rstd[0][:, a:a + 1],
                                             ALU.subtract, ALU.mult)
                last.then_inc(x1_ready, 1)
                dve.wait_ge(x1_ready, c + 1)
                norm_stats(1, x1, c)
            for c in range(CHUNKS):
                affine_norm(1, l1, x1, rows["ln1_w"], rows["ln1_b"], c, l1_ready)
            heads = lambda a, lo, hi: a.rearrange("p (g c) -> p g c", g=KV)[:, :, lo:hi]
            for b in range(NB):
                dve.wait_ge(qkv_kept, 2 * (b // BC) + 2)
                q1 = heads(qkv[:, NB + b, :], 0, 16).rearrange("p g (r d) -> p g r d", r=2)
                if b >= 2:
                    dve.wait_ge(chain, n[0])
                for pos in range(2):
                    k = heads(qkv[:, pos * NB + b, :], 16, 24).unsqueeze(2).broadcast_to([P, KV, 2, DH])
                    last = dve.tensor_tensor(prod[:, b % 2, pos, :].rearrange("p (g r d) -> p g r d", g=KV, r=2),
                                             q1, k, ALU.mult)
                done(last)
                last = dve.tensor_reduce(sc[:, b, :, :], prod[:, b % 2].rearrange("p t (h d) -> p t h d", h=H),
                                         AX.X, ALU.add)
                done(last)
            done(dve.tensor_tensor(sc_max[:], sc[:, :, 0, :], sc[:, :, 1, :], ALU.max))
            for pos in range(2):
                last = dve.tensor_tensor(sc[:, :, pos, :], sc[:, :, pos, :], sc_max[:], ALU.subtract)
            last.then_inc(sc_ready, 1)
            dve.wait_ge(sc_exp, 1)
            done(dve.tensor_tensor(sc_sum[:], sc_e[:, :, 0, :], sc_e[:, :, 1, :], ALU.add))
            done(dve.reciprocal(sc_sum[:], sc_sum[:]))
            for pos in range(2):
                last = dve.tensor_tensor(sc_p[:, :, pos, :], sc_e[:, :, pos, :], sc_sum[:], ALU.mult)
            done(last)
            for b in range(NB):
                for pos in range(2):
                    v = heads(qkv[:, pos * NB + b, :], 24, 32).unsqueeze(2).broadcast_to([P, KV, 2, DH])
                    p_ = sc_p[:, b, pos, :].rearrange("p (g r) -> p g r", g=KV).unsqueeze(3).broadcast_to([P, KV, 2, DH])
                    last = dve.tensor_tensor(mix[:, b % 2, pos, :].rearrange("p (g r d) -> p g r d", g=KV, r=2),
                                             v, p_, ALU.mult)
                done(last)
                dve.tensor_tensor(att[:, NB + b, :], mix[:, b % 2, 0, :], mix[:, b % 2, 1, :],
                                  ALU.add).then_inc(att1_ready, 1)
                dve.wait_ge(att1_ready, b + 1)
            for c in range(CHUNKS):
                dve.wait_ge(p_ready, c + 1)
                dve.tensor_tensor(tiles(hid, c), tiles(x1, c),
                                  ps[:, c, :].rearrange("p (s b d) -> p s b d", s=S, b=BC),
                                  ALU.add).then_inc(hid_ready, 1)
                dve.wait_ge(hid_ready, c + 1)
                norm_stats(2, hid, c)
            for c in range(CHUNKS):
                affine_norm(2, x2, hid, rows["ln2_w"], rows["ln2_b"], c, x2_ready)
            bc = lambda a: a[:].unsqueeze(2).broadcast_to([P, NT, EXPERTS])
            dve.wait_ge(logit_ready, 1)
            lg = ps[:, 0, 0:NT * EXPERTS].rearrange("p (a e) -> p a e", a=NT)
            done(dve.tensor_reduce(lmax[:], lg, AX.X, ALU.max))
            dve.tensor_tensor(logit[:], lg, bc(lmax), ALU.subtract).then_inc(logit_less_max, 1)
            dve.wait_ge(exp_ready, 1)
            done(dve.tensor_reduce(lsum[:], lexp[:], AX.X, ALU.add))
            done(dve.reciprocal(lsum[:], lsum[:]))
            done(dve.tensor_tensor(lprob[:], lexp[:], bc(lsum), ALU.mult))
            dve.wait_ge(ld_const, 48)
            order = expert_rank[:].rearrange("p (a e) -> p a e", a=NT)
            left = lprob
            for k in range(TOP):
                done(dve.tensor_reduce(top[k][:], left[:], AX.X, ALU.max))
                done(dve.tensor_tensor(cand[:], left[:], bc(top[k]), ALU.is_equal))
                done(dve.tensor_tensor(cand[:], cand[:], order, ALU.mult))
                done(dve.tensor_reduce(best[:], cand[:], AX.X, ALU.max))
                done(dve.tensor_tensor(hot[k][:], order, bc(best), ALU.is_equal))
                if k == 0:
                    done(dve.scalar_tensor_tensor(out=rest[:], in0=hot[0][:], scalar=-2.0, in1=lprob[:],
                                                  op0=ALU.mult, op1=ALU.add))
                    left = rest
            dve.tensor_tensor(hot_any[:], hot[0][:], hot[1][:], ALU.add).then_inc(hot_ready, 1)
            done(dve.tensor_tensor(top_sum[:], top[0][:], top[1][:], ALU.add))
            done(dve.reciprocal(top_sum[:], top_sum[:]))
            for k in range(TOP):
                dve.tensor_tensor(weight[k][:], top[k][:], top_sum[:], ALU.mult)
            dve.wait_ge(rank_ready, 1)
            rank = ps[:, 1, 0:P].rearrange("p (a e) -> p a e", a=NT)
            done(dve.tensor_scalar(fits[:], rank, float(CAP), None, ALU.is_lt))
            done(dve.tensor_tensor(slot_of[:], rank, expert_base[:].rearrange("p (a e) -> p a e", a=NT), ALU.add))
            done(dve.tensor_tensor(slot_of[:], slot_of[:], fits[:], ALU.mult))
            done(dve.tensor_scalar(slot_of[:], slot_of[:], float(EXPERTS * CAP), None, ALU.add))
            for k in range(TOP):
                done(dve.tensor_tensor(cand[:], slot_of[:], hot[k][:], ALU.mult))
                done(dve.tensor_reduce(slot_f[:, k, :], cand[:], AX.X, ALU.add))
            dve.tensor_copy(slot_u[:], slot_f[:]).then_inc(slots_ready, 1)


        route.close()
        experts(nc, t, keep, ps)


def experts(nc, t, keep, ps):
    with ExitStack() as ctx:
        def sb(name, shape, dt=F32):
            return ctx.enter_context(nc.sbuf_tensor(name, shape, dt))

        def sem(name):
            return ctx.enter_context(nc.semaphore(name))

        ident, base, slot_u, weight, eps = (keep[k] for k in ("ident", "base", "slot_u", "weight", "eps"))
        xd, yd = t["xd"], t["yd"]
        GROUP = 4
        w1 = [sb(f"w1_{u}", [D, F]) for u in range(2)]
        w2 = [sb(f"w2_{u}", [P, FT, D]) for u in range(2)]
        x_in = [sb(f"x_in{u}", [P, CT, D]) for u in range(2)]
        x_in_t = [sb(f"x_in_t{u}", [D, CAP]) for u in range(2)]
        act_t = [sb(f"act_t{u}", [P, FT, CAP]) for u in range(2)]
        y_out = [sb(f"y_out{u}", [P, CT, D]) for u in range(2)]
        got = [sb(f"got{k}", [P, NT, D]) for k in range(TOP)]
        stats = sb("stats3", [P, NT, 6])
        mv, std, rstd = sb("mv3", [P, NT, 2]), sb("std3", [P, NT]), sb("rstd3", [P, NT])

        loaded = [sem(f"e_loaded{u}") for u in range(2)]
        x_turned, x_kept = sem("e_x_turned"), sem("e_x_kept")
        h_full, h_kept = sem("h_full"), sem("h_kept")
        y_full, y_kept = sem("y_full"), sem("y_kept")
        stored = [sem(f"stored{u}") for u in range(2)]
        gathered = [sem(f"gathered{g}") for g in range(NT // GROUP)]
        chain = sem("chain3")
        var_ready, std_ready, normed, written = sem("var3"), sem("std_ready3"), sem("normed"), sem("written")
        E_ = EXPERTS

        def each_expert(eng, body):
            body(0, 0)
            with eng.Fori(0, (E_ - 4) // 2) as turn:
                for u in (1, 2):
                    body(turn * 2 + u, u % 2)
            for e in range(E_ - 3, E_):
                body(e, e % 2)

        def has(e, ahead):
            return not isinstance(e, int) or e + ahead < E_

        block = ctx.enter_context(nc.Block())

        @block.sync
        def _(sp):
            def load(e, u):
                one = bass.ds(e, 1)
                sp.dma_start(w1[u][:], t["w1"][one].rearrange("o h f -> (o h) f")).then_inc(loaded[u], 16)
                sp.dma_start(w2[u][:], t["w2"][one].rearrange("o (a p) h -> p (o a) h", p=P)).then_inc(loaded[u], 16)
                sp.dma_start(x_in[u][:], xd.rearrange("(e a p) d -> e p a d", a=CT, p=P)[one]
                             .rearrange("o p a d -> (o p) a d")).then_inc(loaded[u], 16)

            load(0, 0)
            load(1, 1)

            def body(e, u):
                if has(e, 2):
                    sp.wait_ge(y_full, e + 1)
                    load(e + 2, u)
                sp.wait_ge(y_kept, e + 1)
                sp.dma_start(yd[0:E_ * CAP, :].rearrange("(e a p) d -> e p a d", a=CT, p=P)[bass.ds(e, 1)]
                             .rearrange("o p a d -> (o p) a d"), y_out[u][:]).then_inc(stored[u], 16)

            each_expert(sp, body)
            for g in range(NT // GROUP):
                sp.wait_ge(normed, g + 1)
                s, blk = g * GROUP // NB, g * GROUP % NB
                sp.dma_start(t["out"][s, blk * P:(blk + GROUP) * P, :].rearrange("(a p) d -> p a d", p=P),
                             base[:, g * GROUP:(g + 1) * GROUP, :]).then_inc(written, 16)
            sp.wait_ge(written, 16 * NT // GROUP)

        @block.gpsimd
        def _(pool):
            for u in range(2):
                pool.wait_ge(stored[u], 16 * E_ // 2)
            for a in range(NT):
                for k in range(TOP):
                    pool.indirect_dma_start(
                        out=got[k][:, a, :], out_offset=None, in_=yd,
                        in_offset=bass.IndirectOffsetOnAxis(ap=slot_u[:, k, a:a + 1], axis=0),
                        bounds_check=E_ * CAP, oob_is_err=False).then_inc(gathered[a // GROUP], 16)

        @block.tensor
        def _(pe):
            def turn_x(e, u):
                pe.wait_ge(loaded[u], (e // 2 + 1) * 48 if isinstance(e, int) else (e - u) * 24 + 48)
                if not (isinstance(e, int) and e < 1):
                    pe.wait_ge(x_kept, e)
                for a in range(CT):
                    mm = pe.transpose(ps[:, a // 4, (a % 4) * P:(a % 4 + 1) * P], x_in[u][:, a, :], ident[:])
                mm.then_inc(x_turned, 1)

            def up(e, u):
                pe.wait_ge(x_kept, e + 1)
                for f in range(FT):
                    if not (isinstance(e, int) and e == 0 and f < 2):
                        pe.wait_ge(h_kept, e * FT + (f - 1))
                    for h in range(2):
                        mm = pe.matmul(ps[:, 2 + 2 * (f % 2) + h, 0:CAP // 2], w1[u][:, f * P:(f + 1) * P],
                                       x_in_t[u][:, h * CAP // 2:(h + 1) * CAP // 2], start=True, stop=True)
                    mm.then_inc(h_full, 1)

            def down(e, u):
                pe.wait_ge(h_kept, e * FT + FT)
                if not (isinstance(e, int) and e < 1):
                    pe.wait_ge(y_kept, e)
                for a in range(CT):
                    for f in range(FT):
                        mm = pe.matmul(ps[:, 6 + a // 4, (a % 4) * P:(a % 4 + 1) * P],
                                       act_t[u][:, f, a * P:(a + 1) * P], w2[u][:, f, :],
                                       start=(f == 0), stop=(f == FT - 1))
                mm.then_inc(y_full, 1)

            turn_x(0, 0)
            up(0, 0)

            def body(e, u):
                if has(e, 1):
                    turn_x(e + 1, 1 - u)
                down(e, u)
                if has(e, 1):
                    up(e + 1, 1 - u)

            each_expert(pe, body)

        @block.scalar
        def _(act):
            def body(e, u):
                for f in range(FT):
                    act.wait_ge(h_full, e * FT + (f + 1))
                    if not (isinstance(e, int) and e < 2) and f == 0:
                        act.wait_ge(y_full, e - 1)
                    act.activation(act_t[u][:, f, :].rearrange("p (h n) -> p h n", h=2),
                                   ps[:, 2 + 2 * (f % 2):4 + 2 * (f % 2), 0:CAP // 2],
                                   ACT.Gelu).then_inc(h_kept, 1)

            body(0, 0)
            body(1, 1)
            with act.Fori(0, (E_ - 2) // 2) as turn:
                for u in range(2):
                    body(turn * 2 + (2 + u), u)
            for g in range(NT // GROUP):
                act.wait_ge(var_ready, g + 1)
                act.activation(std[:, g * GROUP:(g + 1) * GROUP], mv[:, g * GROUP:(g + 1) * GROUP, 1], ACT.Sqrt,
                               bias=eps[:, 0:1]).then_inc(std_ready, 1)

        @block.vector
        def _(dve):
            n = [0]

            def done(ins):
                n[0] += 1
                ins.then_inc(chain, 1)
                dve.wait_ge(chain, n[0])

            def keep_x(e, u):
                dve.wait_ge(x_turned, e + 1)
                if not (isinstance(e, int) and e < 2):
                    dve.wait_ge(h_full, e * FT - FT)
                dve.tensor_copy(x_in_t[u][:], ps[:, 0:2, :].rearrange("p a n -> p (a n)")[:, 0:CAP]).then_inc(x_kept, 1)

            def keep_y(e, u):
                dve.wait_ge(y_full, e + 1)
                if not (isinstance(e, int) and e < 2):
                    dve.wait_ge(stored[u], (e - u) * 8)
                dve.tensor_copy(y_out[u][:].rearrange("p a d -> p (a d)"),
                                ps[:, 6:8, :].rearrange("p a n -> p (a n)")[:, 0:CAP]).then_inc(y_kept, 1)

            keep_x(0, 0)
            keep_x(1, 1)
            keep_y(0, 0)
            keep_x(2, 0)
            keep_y(1, 1)
            keep_x(3, 1)
            with dve.Fori(0, (E_ - 4) // 2) as turn:
                for u in range(2):
                    keep_y(turn * 2 + (2 + u), u)
                    keep_x(turn * 2 + (4 + u), u)
            keep_y(E_ - 2, 0)
            keep_y(E_ - 1, 1)

            for g in range(NT // GROUP):
                dve.wait_ge(gathered[g], 16 * TOP * GROUP)
                for k in range(TOP):
                    for a in range(g * GROUP, (g + 1) * GROUP):
                        last = dve.scalar_tensor_tensor(out=base[:, a, :], in0=got[k][:, a, :],
                                                        scalar=weight[k][:, a:a + 1], in1=base[:, a, :],
                                                        op0=ALU.mult, op1=ALU.add)
                    done(last)
                for a in range(g * GROUP, (g + 1) * GROUP):
                    last = dve.bn_stats(stats[:, a, :], base[:, a, :])
                done(last)
                for a in range(g * GROUP, (g + 1) * GROUP):
                    last = dve.bn_aggr(mv[:, a, :], stats[:, a, :])
                last.then_inc(var_ready, 1)
                dve.wait_ge(std_ready, g + 1)
                done(dve.reciprocal(rstd[:, g * GROUP:(g + 1) * GROUP], std[:, g * GROUP:(g + 1) * GROUP]))
                for a in range(g * GROUP, (g + 1) * GROUP):
                    last = dve.tensor_scalar(base[:, a, :], base[:, a, :], mv[:, a, 0:1], rstd[:, a:a + 1],
                                             ALU.subtract, ALU.mult)
                last.then_inc(normed, 1)


def constants():
    import numpy as np

    def bf16_bits(a):
        return (np.asarray(a, np.float32).view(np.uint32) >> 16).astype(np.uint16)

    n = np.arange(N)
    lo, hi = n % P, n // P * P
    slope = 0.5 ** (np.arange(UNITS) % H)
    block = n // P
    mine = (np.arange(NB)[:, None] == block[None, :]).astype(np.float64)
    sign = np.sign(np.arange(NB)[:, None] - block[None, :])
    alibi_q = np.concatenate([mine, mine, mine * lo])
    alibi_k = slope[:, None, None] * np.concatenate([sign * (hi - P * np.arange(NB)[:, None]), sign * lo, -sign])[None]
    eye = np.eye(P)
    distance = -np.abs(np.arange(P)[:, None] - np.arange(P)[None, :])
    rows, cols = np.arange(P)[:, None], np.arange(P)[None, :]
    experts_ = np.arange(EXPERTS)
    pick = np.zeros((P, 64), np.float32)
    for c in range(4):
        for r in range(DH + 1):
            pick[32 * c + r, 16 * c + r] = 1.0
    return {
        "c_ident": eye.astype(np.float32),
        "c_alibi_q": bf16_bits(alibi_q),
        "c_alibi_k": bf16_bits(alibi_k),
        "c_minus": bf16_bits(-np.ones((PARTS, N))),
        "c_slope_eye": bf16_bits(slope[:, None, None] * eye[None]),
        "c_distance": bf16_bits(distance),
        "c_pick": pick,
        "c_before": bf16_bits(rows < cols),
        "c_experts": np.stack([np.tile(EXPERTS - experts_, NT),
                               np.tile(CAP * experts_ - EXPERTS * CAP, NT)]).astype(np.float32),
    }


def program(nc, t):
    t["qk_dram"] = nc.dram_tensor("qk_dram", [2, UNITS, PARTS, PARTS, DH, N], BF16).ap()
    t["max_dram"] = nc.dram_tensor("max_dram", [2, PARTS, N], BF16).ap()
    t["xd"] = nc.dram_tensor("xd", [EXPERTS * CAP, D], F32).ap()
    t["yd"] = nc.dram_tensor("yd", [EXPERTS * CAP + 1, D], F32).ap()
    with (nc.sbuf_tensor("x_tok", [P, NT, D], F32) as x_tok, nc.sbuf_tensor("ident", [P, P], F32) as ident,
          nc.sbuf_tensor("head_out", [P, NB, UNITS, DH], F32) as head_out):
        keep = {"x_tok": x_tok, "ident": ident, "head_out": head_out}
        attention_and_prep(nc, t, keep)
        second_half(nc, t, keep)


NAMES = {
    "L0_attn_x": "x", "L0_attn_qkv_w": "qkv_w", "L0_attn_qkv_b": "qkv_b", "L0_attn_out_w": "out_w",
    "L0_attn_out_b": "out_b", "L0_ffn_ln1_weight": "ln1_w", "L0_ffn_ln1_bias": "ln1_b",
    "L0_ffn_ln2_weight": "ln2_w", "L0_ffn_ln2_bias": "ln2_b", "L0_ffn_qkv_weight": "qkv_w2",
    "L0_ffn_proj_weight": "proj_w", "L0_ffn_router_weight": "router", "L0_ffn_moe_w1": "w1", "L0_ffn_moe_w2": "w2",
}


def kernel(**inputs):
    import numpy as _np
    import concourse.bacc as _bacc
    from concourse.bass_utils import run_bass_kernel_spmd as _run

    nc = _bacc.Bacc("TRN2", target_bir_lowering=False, num_devices=1)
    arrays, t = {}, {}
    named = {short: inputs[name] for name, short in NAMES.items()}
    for short, value in {**named, **constants()}.items():
        a = _np.ascontiguousarray(value)
        arrays[f"in_{short}"] = a
        ap = nc.dram_tensor(f"in_{short}", a.shape, mybir.dt.from_np(a.dtype), kind="ExternalInput").ap()
        t[short] = ap.bitcast(BF16) if a.dtype == _np.uint16 else ap
    t["out"] = nc.dram_tensor("out_0", [S, N, D], F32, kind="ExternalOutput").ap()
    program(nc, t)
    return _run(nc, [arrays], core_ids=[0]).results[0]["out_0"]
```

```python
from contextlib import ExitStack

import concourse.bass as bass
from concourse import mybir

F32 = mybir.dt.float32
BF16 = mybir.dt.bfloat16
U32 = mybir.dt.uint32
I32 = mybir.dt.int32
ALU = mybir.AluOpType
ACT = mybir.ActivationFunctionType
AX = mybir.AxisListType

P = 128
S = 2
N = 1024
D = 128
H = 16
DH = D // H
NB = N // P
NT = S * NB
UNITS = S * H
HALF = N // 2
QUARTER = N // 4
LAG = 2
SCALE = float(DH) ** -0.5

PARTS = 3
PRODUCTS = PARTS * PARTS * DH
ROW_ALIBI = PRODUCTS
ROW_MAX = ROW_ALIBI + 3 * NB
K_MAX = ROW_MAX
K_EXP = ROW_MAX + PARTS
SLOTS = 4
LOADS = 8


def attention_and_prep(nc, t, keep):
    with ExitStack() as ctx:
        def sb(name, shape, dt=F32):
            return ctx.enter_context(nc.sbuf_tensor(name, shape, dt))

        def sem(name):
            return ctx.enter_context(nc.semaphore(name))

        ps = ctx.enter_context(nc.psum_tensor("ps", [P, 8, 512], F32))

        x_tok, ident, head_out = keep["x_tok"], keep["ident"], keep["head_out"]
        w_nat = sb("w_nat", [P, 3, D])
        w_t = sb("w_t", [D, 3, D])
        x_t = sb("x_t", [D, S * N])
        bias_all = sb("bias_all", [P, H, 3, DH])
        bias_spread = sb("bias_spread", [P, 2, P])
        bias_qk = sb("bias_qk", [P, 2])
        bias_q_scaled = sb("bias_q_scaled", [P, 1])
        proj = sb("proj", [P, 2, 512])
        rest = sb("rest", [P, 2, 512])
        parts = sb("parts", [P, 4, PARTS, 512], BF16)
        v_all = sb("v_all", [P, UNITS, NB, DH + 1])
        q_stacks = sb("q_stacks", [K_EXP, SLOTS, N], BF16)
        k_stacks = sb("k_stacks", [K_EXP, SLOTS, N], BF16)
        q_stack = [q_stacks[:, k, :] for k in range(SLOTS)]
        k_stack = [k_stacks[:, k, :] for k in range(SLOTS)]
        slope_eye = [sb(f"slope_eye{k}", [P, P], BF16) for k in range(SLOTS)]
        v_unit = [sb(f"v_unit{k}", [P, NB, 32]) for k in range(SLOTS)]
        distance = sb("distance", [P, P], BF16)
        pick = sb("pick", [P, 64])
        max_half = sb("max_half", [P, 2, NB, 2])
        row_max = sb("row_max", [P, 2, NB])
        max_t = sb("max_t", [NB, 2, P])
        max_rest = sb("max_rest", [NB, 2, P])
        max_parts = sb("max_parts", [NB, 2, PARTS, P], BF16)
        no_bits = sb("no_bits", [NB, P])
        probs = sb("probs", [P, 4, N])
        out_t = sb("out_t", [P, QUARTER])
        recip = sb("recip", [P, 2, 4])

        ps_s = [ps[:, 0:2, :], ps[:, 2:4, :]]
        ps_m = [ps[:, 4, :], ps[:, 5, :]]
        ps_o = ps[:, 6, 0:QUARTER]
        ps_c = ps[:, 7, :]

        ld_w, ld_bias, ld_const = sem("ld_w"), sem("ld_bias"), sem("ld_const")
        ld_x = [sem(f"ld_x{g}") for g in range(NT // 4)]
        w_turned, w_kept = sem("w_turned"), sem("w_kept")
        x_turned, x_kept = sem("x_turned"), [sem(f"x_kept{s}") for s in range(S)]
        bias_chain, bq_ready = sem("bias_chain"), sem("bq_ready")
        qk_ready, qf_ready, q1_ready, r1_ready, q2_ready, q3_ready = (
            sem("qk_ready"), sem("qf_ready"), sem("q1_ready"), sem("r1_ready"), sem("q2_ready"), sem("q3_ready"))
        parts_saved = [sem(f"parts_saved{b}") for b in range(4)]
        v_ready, v_kept, v_ones = sem("v_ready"), sem("v_kept"), sem("v_ones")
        loaded = [sem(f"loaded{k}") for k in range(SLOTS)]
        max_loaded = [sem(f"max_loaded{k}") for k in range(SLOTS)]
        max_saved = sem("max_saved")
        v_copied = sem("v_copied")
        mx_full, mx_used = sem("mx_full"), sem("mx_used")
        max_done, maxt_full, maxt_kept, split, max_split = (
            sem("max_done"), sem("maxt_full"), sem("maxt_kept"), sem("split"), sem("max_split"))
        s_full, p_ready, pv_done = sem("s_full"), sem("p_ready"), sem("pv_done")
        o_kept, tok_full, recip_done, tok_kept = sem("o_kept"), sem("tok_full"), sem("recip_done"), sem("tok_kept")

        qk_dram = t["qk_dram"]
        max_dram = t["max_dram"]

        TURNS = (UNITS - 4) // SLOTS

        def each_unit(eng, body, lead=2):
            for m in range(lead):
                body(m, m)
            with eng.Fori(0, TURNS) as turn:
                for k in range(lead, lead + SLOTS):
                    body(turn * SLOTS + k, k % SLOTS)
            for m in range(lead + SLOTS * TURNS, UNITS):
                body(m, m % SLOTS)

        def known(m):
            return m if isinstance(m, int) else None

        def first(m):
            return known(m) == 0

        def has_next(m, ahead):
            return known(m) is None or m + ahead < UNITS

        def turn_of(m, slot):
            return (m - slot) // SLOTS + 1

        late_w, late_row, late, late_set = sem("late_w"), sem("late_row"), sem("late"), sem("late_set")
        late_turned, late_kept = sem("late_turned"), sem("late_kept")

        block = ctx.enter_context(nc.Block())

        @block.sync
        def _(sp):
            sp.dma_start(w_nat[:], t["qkv_w"].rearrange("(a p) d -> p a d", p=P)).then_inc(ld_w, 16)
            sp.dma_start(ident[:], t["c_ident"]).then_inc(ld_w, 16)
            for g in range(NT // 4):
                s, blk = 4 * g // NB, 4 * g % NB
                sp.dma_start(x_tok[:, 4 * g:4 * g + 4, :], t["x"][s, blk * P:(blk + 4) * P, :].rearrange(
                    "(a p) d -> p a d", p=P)).then_inc(ld_x[g], 16)
                if g == 0:
                    sp.dma_start(bias_all[:].rearrange("p h c d -> p (h c d)"),
                                 t["qkv_b"].partition_broadcast(P)).then_inc(ld_bias, 16)
            sp.dma_start(distance[:], t["c_distance"]).then_inc(ld_const, 16)
            sp.dma_start(q_stacks[ROW_ALIBI:ROW_MAX, :, :],
                         t["c_alibi_q"].unsqueeze(1).broadcast_to([ROW_MAX - ROW_ALIBI, SLOTS, N])).then_inc(ld_const, 16)
            sp.dma_start(k_stacks[ROW_MAX:K_EXP, :, :],
                         t["c_minus"].unsqueeze(1).broadcast_to([PARTS, SLOTS, N])).then_inc(ld_const, 16)
            sp.dma_start(pick[:], t["c_pick"]).then_inc(ld_const, 16)

            def save(y):
                s, c, half = y // 4, (y // 2) % 2, y % 2
                sp.wait_ge(q3_ready, y + 1)
                sp.dma_start(qk_dram[c, :, s, :, half * 512:(half + 1) * 512].rearrange("a p n -> p a n"),
                             parts[:, y % 4, :, :]).then_inc(parts_saved[y % 4], 16)

            def load_tables(m, slot):
                unit = bass.ds(m, 1)
                sp.dma_start(k_stack[slot][ROW_ALIBI:ROW_MAX, :],
                             t["c_alibi_k"][unit].rearrange("o p n -> (o p) n")).then_inc(loaded[slot], 16)
                sp.dma_start(slope_eye[slot][:],
                             t["c_slope_eye"][unit].rearrange("o p c -> (o p) c")).then_inc(loaded[slot], 16)

            def load_parts(m, slot):
                unit = bass.ds(m, 1)
                for c, stack in ((0, q_stack), (1, k_stack)):
                    if first(m):
                        for y in (2 * c, 2 * c + 1):
                            sp.wait_ge(parts_saved[y], 16)
                    for b in range(PARTS):
                        if c == 0:
                            rows = qk_dram[c].rearrange("a s (h d) n -> (s h) a d n", d=DH)[unit].rearrange(
                                "o a d n -> (o a) d n")
                        else:
                            rows = qk_dram[c, b].rearrange("s (h d) n -> (s h) d n", d=DH)[unit].broadcast_to(
                                [PARTS, DH, N])
                        sp.dma_start(stack[slot][b * PARTS * DH:(b + 1) * PARTS * DH, :],
                                     rows).then_inc(loaded[slot], 16)

            def load_max(m, slot):
                sp.wait_ge(max_split, m + 1)
                b = slot % 2
                sp.dma_start(max_dram[b].rearrange("a (i c) -> i a c", c=P),
                             max_parts[:, b, :, :]).then_inc(max_saved, 16)
                sp.wait_ge(max_saved, 16 * m + 16)
                sp.dma_start(q_stack[slot][ROW_MAX:K_EXP, :], max_dram[b]).then_inc(max_loaded[slot], 16)

            for m in range(3):
                load_tables(m, m)
            for y in range(4):
                save(y)
            for m in range(2):
                load_parts(m, m)
            for y in range(4, 8):
                save(y)
            load_parts(2, 2)
            load_max(0, 0)
            for b in range(4):
                sp.wait_ge(parts_saved[b], 32)

            def body(m, slot):
                if not first(m):
                    sp.wait_ge(s_full, m * NB)
                if has_next(m, 3):
                    load_tables(m + 3, (slot + 3) % 4)
                    load_parts(m + 3, (slot + 3) % 4)
                if has_next(m, 1):
                    load_max(m + 1, (slot + 1) % 4)

            each_unit(sp, body, lead=1)

        def fetch_late(pool):
            pool.memset(keep["ones"][:], 1.0)
            pool.memset(keep["zeros"][:], 0.0).then_inc(late_set, 1)
            pool.memset(keep["blank"][:], 0.0).then_inc(late_set, 1)
            pool.wait_ge(late_set, 2)
            pool.memset(keep["blank"][:, :, TO:TO + 1], float(TOP * NT * P)).then_inc(late_set, 1)
            with nc.allow_non_contiguous_dma(reason="one value per partition"):
                for i, n in enumerate(("ln1_w", "ln1_b", "ln2_w", "ln2_b")):
                    pool.dma_start(keep["ln"][:, i:i + 1], t[n].rearrange("(d o) -> d o", o=1)).then_inc(late, 16)
            pool.dma_start(keep["router"][:], t["router"]).then_inc(late, 16)
            pool.dma_start(keep["before"][:], t["c_before"]).then_inc(late, 16)
            pool.dma_start(keep["expert_rank"][:], t["c_experts"][0].partition_broadcast(P)).then_inc(late, 16)
            pool.dma_start(keep["expert_base"][:], t["c_experts"][1].partition_broadcast(P)).then_inc(late, 16)
            pool.dma_start(keep["to_row"][:], t["c_to_row"]).then_inc(late, 16)
            for u in range(2):
                pool.dma_start(keep["w1"][u][:], t["w1"][u]).then_inc(late, 16)
                pool.dma_start(keep["w2"][u][:], t["w2"][u].rearrange("(a p) h -> p a h", p=P)).then_inc(late, 16)
            pool.wait_ge(late_set, 3)
            for e in range(EXPERTS):
                pool.dma_start(t["xd"][e * CAP:(e + 1) * CAP, :].rearrange("(p a) w -> p (a w)", p=P),
                               keep["blank"][:].rearrange("p a w -> p (a w)")).then_inc(late, 16)
            rows = 8 * P
            for i in range(TOP * NT * P // rows):
                pool.dma_start(t["yt"][i * rows:(i + 1) * rows, :].rearrange("(p a) d -> p (a d)", p=P),
                               keep["zeros"][:]).then_inc(late, 16)

        @block.gpsimd
        def _(pool):
            pool.dma_start(keep["wo_nat"][:], t["out_w"]).then_inc(late_w, 16)
            pool.dma_start(keep["wq_nat"][:], t["qkv_w2"].rearrange("(a p) d -> p a d", p=P)).then_inc(late_w, 16)
            pool.dma_start(keep["wp_nat"][:], t["proj_w"]).then_inc(late_w, 16)
            pool.dma_start(keep["out_b"][:], t["out_b"].partition_broadcast(P)).then_inc(late_row, 16)
            pool.memset(v_all[:], 1.0).then_inc(v_ones, 1)
            for k in range(SLOTS):
                pool.memset(v_unit[k][:], 0.0).then_inc(v_ones, 1)
            pool.memset(no_bits[:], 0.0).then_inc(v_ones, 1)
            pool.wait_ge(v_ones, 2 + SLOTS)
            fetch_late(pool)
            pool.wait_ge(late_row, 16)
            pool.wait_ge(x_turned, NT // 4)
            pool.tensor_tensor(x_tok[:], x_tok[:], keep["out_b"][:].unsqueeze(1).broadcast_to([P, NT, D]), ALU.add)

            def copy_v(m, slot):
                pool.tensor_copy(v_unit[slot][:, :, 0:DH + 1],
                                 v_all[:, bass.ds(m, 1), :, :].rearrange("p o a c -> p (o a) c")).then_inc(v_copied, 1)

            def split_max(m, slot):
                b = slot % 2
                src, rst, out = max_t[:, b, :], max_rest[:, b, :], max_parts[:, b, :, :]
                pool.wait_ge(maxt_kept, m + 1)
                if not (isinstance(m, int) and m < 2):
                    pool.wait_ge(max_saved, 16 * m - 16)
                pool.tensor_tensor(out[:, 0, :], src, no_bits[:], ALU.add).then_inc(split, 1)
                pool.wait_ge(split, 3 * m + 1)
                pool.tensor_tensor(rst, src, out[:, 0, :], ALU.subtract).then_inc(split, 1)
                pool.wait_ge(split, 3 * m + 2)
                pool.tensor_tensor(out[:, 1, :], rst, no_bits[:], ALU.add).then_inc(split, 1)
                pool.wait_ge(split, 3 * m + 3)
                pool.tensor_tensor(out[:, 2, :], rst, out[:, 1, :], ALU.subtract).then_inc(max_split, 1)

            pool.wait_ge(v_kept, NT // 4)
            copy_v(0, 0)
            copy_v(1, 1)
            split_max(0, 0)

            def body(m, slot):
                if has_next(m, 2) and not (known(m) is not None and m < 2):
                    pool.wait_ge(pv_done, NB * m - NB)
                if has_next(m, 1):
                    split_max(m + 1, (slot + 1) % 4)
                if has_next(m, 2):
                    copy_v(m + 2, (slot + 2) % 4)

            each_unit(pool, body)
            pool.wait_ge(late, 16 * LATE_DMAS)

        @block.tensor
        def _(pe):
            pe.wait_ge(ld_w, 32)
            for a in range(3):
                mm = pe.transpose(ps[:, 0, a * P:(a + 1) * P], w_nat[:, a, :], ident[:])
            mm.then_inc(w_turned, 1)
            for g in range(4):
                pe.wait_ge(ld_x[g], 16)
                for j in range(4):
                    mm = pe.transpose(ps[:, 1 + g, j * P:(j + 1) * P], x_tok[:, 4 * g + j, :], ident[:])
                mm.then_inc(x_turned, 1)
            pe.wait_ge(w_kept, 3)
            for y in range(8):
                s, c, half = y // 4, (y // 2) % 2, y % 2
                g = s * 2 + half
                pe.wait_ge(x_kept[g // 2], g % 2 + 1)
                if y >= 3:
                    pe.wait_ge(qf_ready, y - 2)
                pe.matmul(ps[:, 5 + y % 3, :], w_t[:, c, :], x_t[:, g * 512:(g + 1) * 512],
                          start=True, stop=True).then_inc(qk_ready, 1)
                if y % 2 == 1:
                    gv = y // 2
                    for j in range(4):
                        tile = 4 * gv + j
                        mm = pe.matmul(ps[:, 1 + gv, j * P:(j + 1) * P], x_t[:, tile * P:(tile + 1) * P],
                                       w_t[:, 2, :], start=True, stop=True)
                    mm.then_inc(v_ready, 1)

            def scores(out, rows, stack, rhs, slot, block, h):
                on_diagonal = block // 4 == h
                mm = pe.matmul(out, stack[slot][0:rows, block * P:(block + 1) * P],
                               rhs[slot][0:rows, HALF * h:HALF * (h + 1)], start=True, stop=not on_diagonal)
                if on_diagonal:
                    a = P * (block % 4)
                    mm = pe.matmul(out[:, a:a + P], slope_eye[slot][:], distance[:], start=False, stop=True)
                return mm

            def max_bank(m, slot, i, h):
                if not (isinstance(m, int) and m == 0 and i == 0):
                    pe.wait_ge(mx_used, 16 * m + (2 * i + h - 1))
                scores(ps_m[h], K_MAX, q_stack, k_stack, slot, i, h).then_inc(mx_full, 1)

            def exp_bank(slot, j, h, which):
                return scores(ps_s[which][:, h, :], K_EXP, k_stack, q_stack, slot, j, h)

            def turn_max(m, slot):
                pe.wait_ge(max_done, m + 1)
                if not (isinstance(m, int) and m < 1):
                    pe.wait_ge(maxt_kept, m)
                pe.transpose(ps_c[0:NB, P:2 * P], row_max[:, slot % 2, :], ident[:]).then_inc(maxt_full, 1)

            def values(m, slot, j):
                pe.wait_ge(p_ready, m * NB + (j + 1))
                if j == 0:
                    pe.wait_ge(v_copied, m + 1)
                    if not first(m):
                        pe.wait_ge(o_kept, m)
                for c in range(4):
                    mm = pe.matmul(ps_o[32 * c:32 * c + 32, :], v_unit[slot][:, j, :],
                                   probs[:, j % 4, QUARTER * c:QUARTER * (c + 1)],
                                   start=(j == 0), stop=(j == NB - 1), tile_position=(0, 32 * c))
                mm.then_inc(pv_done, 1)

            def to_tokens(m):
                pe.wait_ge(o_kept, m + 1)
                for b in range(2):
                    mm = pe.matmul(ps_c[:, 64 * b:64 * b + 64], out_t[:, b * P:(b + 1) * P], pick[:],
                                   start=True, stop=True)
                mm.then_inc(tok_full, 1)

            pe.wait_ge(late_w, 48)
            pe.transpose(ps[:, 0, 0:P], keep["wo_nat"][:], ident[:])
            for a in range(2):
                pe.transpose(ps[:, 0, (1 + a) * P:(2 + a) * P], keep["wq_nat"][:, a, :], ident[:])
            pe.transpose(ps[:, 0, 3 * P:4 * P], keep["wp_nat"][:], ident[:]).then_inc(late_turned, 1)
            pe.wait_ge(ld_const, 16 * 4)
            pe.wait_ge(late_kept, 5)
            pe.wait_ge(qf_ready, 8)
            pe.wait_ge(v_kept, 4)
            for m in range(2):
                pe.wait_ge(loaded[m], 16 * LOADS)
                for i in range(NB):
                    for h in range(2):
                        max_bank(m, m, i, h)
                if m == 0:
                    turn_max(0, 0)

            def body(m, slot):
                nxt = (slot + 2) % 4
                for j in range(NB):
                    if j == 0:
                        pe.wait_ge(max_loaded[slot], turn_of(m, slot) * 16)
                        if has_next(m, 2):
                            pe.wait_ge(loaded[nxt], turn_of(m + 2, nxt) * (16 * LOADS))
                    if not (first(m) and j < 2):
                        pe.wait_ge(p_ready, m * NB + (j - 1))
                    if has_next(m, 2):
                        max_bank(m + 2, nxt, j, 0)
                    for h in range(2):
                        mm = exp_bank(slot, j, h, j % 2)
                    mm.then_inc(s_full, 1)
                    if has_next(m, 2):
                        max_bank(m + 2, nxt, j, 1)
                    if j >= LAG:
                        values(m, slot, j - LAG)
                    elif not first(m):
                        values(m - 1, (slot - 1) % 4, NB - LAG + j)
                    if j == 1 and has_next(m, 1):
                        if not (known(m) is not None and m < 2):
                            pe.wait_ge(tok_kept, m - 1)
                        turn_max(m + 1, (slot + 1) % 4)
                    if j == 4 and not first(m):
                        if has_next(m, 1):
                            pe.wait_ge(maxt_kept, m + 2)
                        else:
                            pe.wait_ge(tok_kept, m - 1)
                        to_tokens(m - 1)

            each_unit(pe, body)
            for j in range(NB - LAG, NB):
                values(UNITS - 1, (UNITS - 1) % 4, j)
            pe.wait_ge(tok_kept, UNITS - 1)
            to_tokens(UNITS - 1)

        @block.scalar
        def _(act):
            for g in range(2):
                act.wait_ge(x_turned, g + 1)
                act.copy(x_t[:, g * 512:(g + 1) * 512], ps[:, 1 + g, :]).then_inc(x_kept[g // 2], 1)
            act.wait_ge(bq_ready, 2)

            def second_part(y):
                act.wait_ge(r1_ready, y + 1)
                act.copy(parts[:, y % 4, 1, :], rest[:, y % 2, :]).then_inc(q2_ready, 1)

            for y in range(8):
                c = (y // 2) % 2
                b = y % 2
                act.wait_ge(qk_ready, y + 1)
                if y >= 2:
                    act.wait_ge(r1_ready, y - 1)
                act.activation(proj[:, b, :], ps[:, 5 + y % 3, :], ACT.Identity,
                               bias=(bias_q_scaled[:, 0:1] if c == 0 else bias_qk[:, 1:2]),
                               scale=(SCALE if c == 0 else 1.0)).then_inc(qf_ready, 1)
                act.wait_ge(qf_ready, y + 1)
                if y >= 4:
                    act.wait_ge(parts_saved[y % 4], 16)
                act.copy(parts[:, y % 4, 0, :], proj[:, b, :]).then_inc(q1_ready, 1)
                if y >= 1:
                    second_part(y - 1)
            second_part(7)

            def keep_max(m, slot):
                act.wait_ge(maxt_full, m + 1)
                if not (isinstance(m, int) and m < 2):
                    act.wait_ge(max_split, m - 1)
                act.copy(max_t[:, slot % 2, :], ps_c[0:NB, P:2 * P]).then_inc(maxt_kept, 1)

            def keep_out(m):
                act.wait_ge(pv_done, NB * m + NB)
                if not first(m):
                    act.wait_ge(tok_full, m)
                act.copy(out_t[:], ps_o).then_inc(o_kept, 1)

            keep_max(0, 0)

            def body(m, slot):
                for j in range(NB):
                    act.wait_ge(s_full, m * NB + (j + 1))
                    if not (first(m) and j < 4):
                        act.wait_ge(pv_done, NB * m + (j - 3))
                    act.activation(probs[:, j % 4, :], ps_s[j % 2].rearrange("p a n -> p (a n)"),
                                   ACT.Exp).then_inc(p_ready, 1)
                    if j == 1 and not first(m):
                        keep_out(m - 1)
                    if j == 2 and has_next(m, 1):
                        keep_max(m + 1, (slot + 1) % 4)

            each_unit(act, body)
            keep_out(UNITS - 1)

        @block.vector
        def _(dve):
            dve.wait_ge(w_turned, 1)
            for c in range(3):
                dve.tensor_copy(w_t[:, c, :].rearrange("p (h d) -> p h d", h=H),
                                ps[:, 0, 0:3 * D].rearrange("p (h c d) -> p c h d", h=H, c=3)[:, c]
                                ).then_inc(w_kept, 1)
            dve.wait_ge(ld_bias, 16)
            dve.wait_ge(ld_w, 32)
            for c in range(2):
                dve.tensor_tensor(bias_spread[:, c, :].rearrange("p (h d) -> p h d", h=H), bias_all[:, :, c, :],
                                  ident[:].rearrange("p (h d) -> p h d", h=H), ALU.mult).then_inc(bias_chain, 1)
            dve.wait_ge(bias_chain, 2)
            dve.tensor_reduce(bias_qk[:], bias_spread[:], AX.X, ALU.add).then_inc(bq_ready, 1)
            dve.wait_ge(bq_ready, 1)
            dve.tensor_scalar(bias_q_scaled[:], bias_qk[:, 0:1], SCALE, None, ALU.mult).then_inc(bq_ready, 1)
            dve.wait_ge(v_ones, 1)
            for g in range(2, 4):
                dve.wait_ge(x_turned, g + 1)
                dve.tensor_copy(x_t[:, g * 512:(g + 1) * 512], ps[:, 1 + g, :]).then_inc(x_kept[g // 2], 1)

            def third_part(y):
                dve.wait_ge(q2_ready, y + 1)
                dve.wait_ge(r1_ready, y + 1)
                dve.tensor_tensor(parts[:, y % 4, 2, :], rest[:, y % 2, :], parts[:, y % 4, 1, :],
                                  ALU.subtract).then_inc(q3_ready, 1)

            for y in range(8):
                b = y % 2
                dve.wait_ge(q1_ready, y + 1)
                if y >= 2:
                    dve.wait_ge(q3_ready, y - 1)
                dve.tensor_tensor(rest[:, b, :], proj[:, b, :], parts[:, y % 4, 0, :], ALU.subtract).then_inc(r1_ready, 1)
                if y >= 1:
                    third_part(y - 1)
                if y % 2 == 1:
                    gv = y // 2
                    s, blk = gv // 2, 4 * (gv % 2)
                    dve.wait_ge(v_ready, gv + 1)
                    for a in range(4):
                        last = dve.tensor_tensor(
                            v_all[:, s * H:(s + 1) * H, blk + a, 0:DH],
                            ps[:, 1 + gv, a * P:(a + 1) * P].rearrange("p (h d) -> p h d", h=H),
                            bias_all[:, :, 2, :], ALU.add)
                    last.then_inc(v_kept, 1)
            third_part(7)

            dve.wait_ge(late_turned, 1)
            dve.tensor_copy(keep["wo_t"][:], ps[:, 0, 0:P]).then_inc(late_kept, 1)
            dve.tensor_copy(keep["wq_t"][:], ps[:, 0, P:3 * P]).then_inc(late_kept, 1)
            dve.tensor_copy(keep["wp_t"][:], ps[:, 0, 3 * P:4 * P]).then_inc(late_kept, 1)
            for r in range(2):
                dve.tensor_copy(keep["wv_t"][:].rearrange("p (g r d) -> p g r d", g=KV, r=2)[:, :, r],
                                ps[:, 0, P:3 * P].rearrange("p (g c) -> p g c", g=KV)[:, :, 24:32]
                                ).then_inc(late_kept, 1)

            def reduce_bank(m, slot, g):
                dve.wait_ge(mx_full, 16 * m + (g + 1))
                dve.tensor_reduce(max_half[:, slot % 2, g // 2, g % 2:g % 2 + 1], ps_m[g % 2],
                                  AX.X, ALU.max).then_inc(mx_used, 1)

            def join_max(m, slot):
                dve.wait_ge(mx_used, 16 * m + 16)
                if not (isinstance(m, int) and m < 2):
                    dve.wait_ge(maxt_full, m - 1)
                dve.tensor_reduce(row_max[:, slot % 2, :], max_half[:, slot % 2, :, :], AX.X,
                                  ALU.max).then_inc(max_done, 1)

            def keep_tokens(m):
                v = ps_c[:, 0:P].rearrange("p (b c r) -> p b c r", b=2, c=4)
                dve.wait_ge(tok_full, m + 1)
                if not first(m):
                    dve.wait_ge(tok_kept, m)
                dve.reciprocal(recip[:], v[:, :, :, DH]).then_inc(recip_done, 1)
                dve.wait_ge(recip_done, m + 1)
                out = head_out[:, :, bass.ds(m, 1), :].rearrange("p (c b) o d -> p b c (o d)", b=2)
                dve.tensor_tensor(out, v[:, :, :, 0:DH], recip[:].unsqueeze(3).broadcast_to([P, 2, 4, DH]),
                                  ALU.mult).then_inc(tok_kept, 1)

            for m in range(2):
                for g in range(16):
                    reduce_bank(m, m, g)
                join_max(m, m)

            def body(m, slot):
                if has_next(m, 2):
                    dve.wait_ge(max_done, m + 1)
                for g in range(16):
                    if has_next(m, 2):
                        reduce_bank(m + 2, (slot + 2) % 4, g)
                    if g == 9 and not first(m):
                        keep_tokens(m - 1)
                if has_next(m, 2):
                    join_max(m + 2, (slot + 2) % 4)

            each_unit(dve, body)
            keep_tokens(UNITS - 1)


EXPERTS = 8
TOP = 2
CAP = 640
CT = CAP // P
F = 512
FT = F // P
KV = 8
QKV = 256
TC = 4
CHUNKS = NT // TC
PER_S = CHUNKS // S
TS = NT // S
EPS = 1e-5
LAST_BANKS = (6, 7, 2, 3, 4)
XW = D + 2
TO = D
WEIGHT = D + 1
LATE_DMAS = 9 + 4 + EXPERTS + TOP * NT // 8

(TURN_HEADS, PROJECT, ROOT0, NORM0, ROOT1, NORM1, KEEP_L, QKV_KEPT, MIX, PROJECT2, ROOT2, NORM2,
 LOGITS, EXP_LOGITS, ROUTE) = range(15)
STAGES = ROUTE + 1
STARTS = (0, 1, 1, 2)


def each_stage(run):
    for step in range(STAGES + max(STARTS)):
        for c in range(CHUNKS):
            if 0 <= step - STARTS[c] < STAGES:
                run(step - STARTS[c], c)


def late_buffers(sb):
    return {
        "wo_nat": sb("wo_nat", [P, D]), "wq_nat": sb("wq_nat", [P, 2, D]), "wp_nat": sb("wp_nat", [P, D]),
        "wo_t": sb("wo_t", [D, D]), "wq_t": sb("wq_t", [D, QKV]), "wp_t": sb("wp_t", [D, D]),
        "wv_t": sb("wv_t", [D, D]),
        "out_b": sb("out_b_row", [P, D]),
        "router": sb("router", [D, EXPERTS]),
        "ln": sb("ln_columns", [D, 4]),
        "before": sb("before", [P, P], BF16),
        "expert_rank": sb("expert_rank", [P, TS * EXPERTS]),
        "expert_base": sb("expert_base", [P, TS * EXPERTS]),
        "to_row": sb("to_row", [P, TOP, NT]),
        "ones": sb("ones", [P, P], BF16),
        "zeros": sb("zeros", [P, 8 * D]),
        "blank": sb("blank", [P, CT, XW]),
        "w1": [sb(f"w1_{u}", [D, F]) for u in range(2)],
        "w2": [sb(f"w2_{u}", [P, FT, D]) for u in range(2)],
    }


def second_half(nc, t, keep):
    with ExitStack() as ctx:
        def sb(name, shape, dt=F32):
            return ctx.enter_context(nc.sbuf_tensor(name, shape, dt))

        def sem(name):
            return ctx.enter_context(nc.semaphore(name))

        ps = ctx.enter_context(nc.psum_tensor("ps2", [P, 8, 512], F32))
        x_tok, ident, head_out = keep["x_tok"], keep["ident"], keep["head_out"]
        wo_t, wq_t, wp_t, router, ln = (keep[k] for k in ("wo_t", "wq_t", "wp_t", "router", "ln"))
        before, ones, w1, w2 = (keep[k] for k in ("before", "ones", "w1", "w2"))

        turned = sb("turned", [P, CHUNKS, TC * P])
        x1 = sb("x1", [P, NT, D])
        l1 = sb("l1", [P, NT, D])
        qkv = sb("qkv", [P, NT, QKV])
        att = sb("att", [P, NT, D])
        hid = sb("hid", [P, NT, D])
        base = sb("base", [P, NT, D])
        row_of = [sb(f"row_of{k}", [P, NT, XW]) for k in range(TOP)]
        stats = sb("stats", [P, NT, 6])
        mv = [sb(f"mv{i}", [P, NT, 2]) for i in range(4)]
        var_eps = [sb(f"var_eps{i}", [P, NT]) for i in range(4)]
        rstd = [sb(f"rstd{i}", [P, NT]) for i in range(4)]
        shift = [sb(f"shift{i}", [P, NT]) for i in range(4)]
        prod = sb("prod", [P, TC, 2, D])
        mix = sb("mix", [P, TC, 2, D])
        sc = [sb(f"sc{c}", [P, TC, 2, H]) for c in range(PER_S)]
        sc_max = sb("sc_max", [P, TC, H])
        sc_e = [sb(f"sc_e{c}", [P, TC, 2, H]) for c in range(PER_S)]
        sc_sum = sb("sc_sum", [P, TC, H])
        sc_p = sb("sc_p", [P, TC, 2, H])
        logit = sb("logit", [P, NT, EXPERTS])
        lmax = sb("lmax", [P, NT])
        lexp = sb("lexp", [P, NT, EXPERTS])
        lsum = sb("lsum", [P, TS])
        lprob = sb("lprob", [P, TS, EXPERTS])
        rest = sb("rest2", [P, TS, EXPERTS])
        cand = sb("cand", [P, TS, EXPERTS])
        best = sb("best", [P, TS])
        top = [sb(f"top{k}", [P, TS]) for k in range(TOP)]
        hots = sb("hots", [P, TOP, TS * EXPERTS])
        hot = [hots[:, k, :].rearrange("p (a e) -> p a e", e=EXPERTS) for k in range(TOP)]
        hot_any = sb("hot_any", [P, NT, EXPERTS], BF16)
        fits = sb("fits", [P, TS * EXPERTS])
        slot_of = sb("slot_of", [P, PER_S, TC * EXPERTS])
        picked = sb("picked", [P, TOP, TS * EXPERTS])
        slot_f = sb("slot_f", [P, TOP * TS])
        slot_u = [sb(f"slot_u{s}", [P, TOP, TS], U32) for s in range(S)]
        top_sum = sb("top_sum", [P, TS])
        x_in = [sb(f"x_in{u}", [P, CT, XW]) for u in range(2)]
        columns = [sb(f"columns{u}", [P, CT, 2]) for u in range(2)]
        x_in_t = [sb(f"x_in_t{u}", [D, CAP]) for u in range(2)]
        act_t = [sb(f"act_t{u}", [P, FT, CAP]) for u in range(2)]
        y_out = [sb(f"y_out{u}", [P, CT, D]) for u in range(2)]
        y_to = [sb(f"y_to{u}", [P, CT], U32) for u in range(2)]
        got = sb("got", [P, NT, TOP * D])
        minus_half = sb("minus_half", [P, TC])

        chain = sem("chain")
        heads_turned, heads_kept = sem("heads_turned"), sem("heads_kept")
        a_ready, a_summed = sem("a_ready"), sem("a_summed")
        half_set, var_raised = sem("half_set"), [sem(f"var_raised{i}") for i in range(4)]
        var_ready, rstd_ready, scale_ready = ([sem(f"{n}{i}") for i in range(4)]
                                             for n in ("var_ready", "rstd_ready", "scale_ready"))
        x1_ready, l1_ready = sem("x1_ready"), sem("l1_ready")
        l_turned, l_kept = sem("l_turned"), sem("l_kept")
        qkv_ready, qkv_kept = sem("qkv_ready2"), sem("qkv_kept")
        sc_ready, sc_exp, att1_ready = sem("sc_ready"), sem("sc_exp"), sem("att1_ready")
        att_turned, att_kept = sem("att_turned"), sem("att_kept")
        p_ready, hid_ready, base_ready = sem("proj_ready"), sem("hid_ready"), sem("base_ready")
        x2_ready, x2_turned, x2_kept, rows_ready = sem("x2_ready"), sem("x2_turned"), sem("x2_kept"), sem("rows_ready")
        logit_ready, logit_less_max, exp_ready = sem("logit_ready"), sem("logit_less_max"), sem("exp_ready")
        hot_ready, rank_ready, slots_ready = sem("hot_ready"), sem("rank_ready"), sem("slots_ready")
        scattered = sem("scattered")
        w_loaded = [sem(f"w_loaded{u}") for u in range(2)]
        x_loaded = [sem(f"x_loaded{u}") for u in range(2)]
        e_turned, e_kept = sem("e_turned"), sem("e_kept")
        h_full, h_kept = sem("h_full"), sem("h_kept")
        y_full, y_kept = sem("y_full"), sem("y_kept")
        tile_full, tile_kept = sem("tile_full"), sem("tile_kept")
        y_sent = [sem(f"y_sent{u}") for u in range(2)]
        fetched = [sem(f"fetched{g}") for g in range(CHUNKS)]
        normed, written = sem("normed"), sem("written")

        xd, yt = t["xd"], t["yt"]
        E_ = EXPERTS
        block = ctx.enter_context(nc.Block())

        def tiles(c):
            return range(TC * c, TC * (c + 1))

        def chunk(c):
            return slice(TC * c, TC * (c + 1))

        def each_expert(eng, body):
            body(0, 0)
            with eng.Fori(0, (E_ - 4) // 2) as turn:
                for u in (1, 2):
                    body(turn * 2 + u, u % 2)
            for e in range(E_ - 3, E_):
                body(e, e % 2)

        def has(e, ahead):
            return not isinstance(e, int) or e + ahead < E_

        @block.sync
        def _(sp):
            def load_w(e, u):
                one = bass.ds(e, 1)
                sp.dma_start(w1[u][:], t["w1"][one].rearrange("o h f -> (o h) f")).then_inc(w_loaded[u], 16)
                sp.dma_start(w2[u][:], t["w2"][one].rearrange("o (a p) h -> p (o a) h", p=P)).then_inc(w_loaded[u], 16)

            def load_x(e, u):
                sp.dma_start(x_in[u][:], xd.rearrange("(e a p) w -> e p a w", a=CT, p=P)[bass.ds(e, 1)]
                             .rearrange("o p a w -> (o p) a w")).then_inc(x_loaded[u], 16)

            sp.wait_ge(scattered, 16 * TOP * NT)
            load_x(0, 0)
            load_x(1, 1)

            def body(e, u):
                if has(e, 2):
                    sp.wait_ge(e_kept, e + 1)
                    load_x(e + 2, u)
                    sp.wait_ge(y_full, e + 1)
                    load_w(e + 2, u)

            each_expert(sp, body)
            for u in range(2):
                sp.wait_ge(y_sent[u], 16 * CT * E_ // 2)
            for g in range(CHUNKS):
                sp.dma_start(got[:, chunk(g), :], yt.rearrange("(a p k) d -> p a (k d)", p=P, k=TOP)[:, chunk(g), :]
                             ).then_inc(fetched[g], 16)
            for g in range(CHUNKS):
                sp.wait_ge(normed, g + 1)
                s, blk = TC * g // NB, TC * g % NB
                sp.dma_start(t["out"][s, blk * P:(blk + TC) * P, :].rearrange("(a p) d -> p a d", p=P),
                             base[:, chunk(g), :]).then_inc(written, 16)
            sp.wait_ge(written, 16 * CHUNKS)

        @block.gpsimd
        def _(pool):
            for k in range(TOP):
                pool.tensor_copy(row_of[k][:, :, TO], keep["to_row"][:, k, :]).then_inc(rows_ready, 1)

            pool.memset(minus_half[:], -0.5).then_inc(half_set, 1)
            pool.wait_ge(half_set, 1)

            def inverse_root(i, c):
                pool.wait_ge(var_ready[i], c + 1)
                pool.tensor_scalar(var_eps[i][:, chunk(c)], mv[i][:, chunk(c), 1], EPS, None, ALU.add).then_inc(var_raised[i], 1)
                pool.wait_ge(var_raised[i], c + 1)
                pool.tensor_tensor(rstd[i][:, chunk(c)], var_eps[i][:, chunk(c)], minus_half[:],
                                   ALU.pow).then_inc(rstd_ready[i], 1)

            def run(stage, c):
                s = c // PER_S
                if stage in (ROOT0, ROOT1, ROOT2):
                    inverse_root((ROOT0, ROOT1, ROOT2).index(stage), c)
                if stage == LOGITS:
                    pool.wait_ge(x2_ready, c + 1)
                    pool.tensor_copy(row_of[1][:, chunk(c), 0:D], row_of[0][:, chunk(c), 0:D]).then_inc(rows_ready, 1)
                if stage == ROUTE and c % PER_S == PER_S - 1:
                    pool.wait_ge(rows_ready, TOP + c + 1)
                    pool.wait_ge(slots_ready, s + 1)
                    for k in range(TOP):
                        for a in range(TS):
                            pool.indirect_dma_start(
                                out=xd, out_offset=bass.IndirectOffsetOnAxis(ap=slot_u[s][:, k, a:a + 1], axis=0),
                                in_=row_of[k][:, TS * s + a, :], in_offset=None, bounds_check=E_ * CAP - 1,
                                oob_is_err=False).then_inc(scattered, 16)

            each_stage(run)
            for c in range(CHUNKS):
                pool.wait_ge(hid_ready, c + 1)
                pool.tensor_tensor(base[:, chunk(c), :], hid[:, chunk(c), :], x1[:, chunk(c), :],
                                   ALU.add).then_inc(base_ready, 1)

            def body(e, u):
                for a in range(CT):
                    if e == E_ - 1:
                        pool.wait_ge(tile_kept, a + 1)
                    elif a == 0:
                        pool.wait_ge(y_kept, e + 1)
                    pool.indirect_dma_start(
                        out=yt, out_offset=bass.IndirectOffsetOnAxis(ap=y_to[u][:, a:a + 1], axis=0),
                        in_=y_out[u][:, a, :], in_offset=None, bounds_check=TOP * NT * P - 1,
                        oob_is_err=False).then_inc(y_sent[u], 16)

            for e in range(E_):
                body(e, e % 2)
            for c in range(CHUNKS):
                inverse_root(3, c)

        @block.tensor
        def _(pe):
            def run(stage, c):
                s = c // PER_S
                if stage == TURN_HEADS:
                    for j, a in enumerate(tiles(c)):
                        mm = pe.transpose(ps[:, c, j * P:(j + 1) * P],
                                          head_out[:, a % NB, s * H:(s + 1) * H, :], ident[:])
                    mm.then_inc(heads_turned, 1)
                if stage == PROJECT:
                    pe.wait_ge(heads_kept, c + 1)
                    for j in range(TC):
                        mm = pe.matmul(ps[:, 4 + c, j * P:(j + 1) * P], turned[:, c, j * P:(j + 1) * P], wo_t[:],
                                       start=True, stop=True)
                    mm.then_inc(a_ready, 1)
                if stage == NORM1:
                    pe.wait_ge(l1_ready, c + 1)
                    for j, a in enumerate(tiles(c)):
                        mm = pe.transpose(ps[:, c, j * P:(j + 1) * P], l1[:, a, :], ident[:])
                    mm.then_inc(l_turned, 1)
                if stage == KEEP_L:
                    pe.wait_ge(l_kept, c + 1)
                    pe.wait_ge(a_summed, c + 1)
                    for j in range(TC):
                        bank = 4 + c if j < 2 else c
                        mm = pe.matmul(ps[:, bank, (j % 2) * QKV:(j % 2 + 1) * QKV], turned[:, c, j * P:(j + 1) * P],
                                       wq_t[:], start=True, stop=True)
                        if j % 2 == 1:
                            mm.then_inc(qkv_ready, 1)
                if stage == MIX:
                    pe.wait_ge(qkv_kept, 2 * c + 2)
                    if s == 0:
                        mm = pe.matmul(ps[:, 4 + c, :], keep["wv_t"][:], turned[:, c, :], start=True, stop=True)
                    else:
                        pe.wait_ge(att1_ready, c % PER_S + 1)
                        for j, a in enumerate(tiles(c)):
                            mm = pe.transpose(ps[:, 4 + c, j * P:(j + 1) * P], att[:, a, :], ident[:])
                    mm.then_inc(att_turned, 1)
                if stage == PROJECT2:
                    pe.wait_ge(att_kept, c + 1)
                    for j in range(TC):
                        mm = pe.matmul(ps[:, c, j * P:(j + 1) * P], turned[:, c, j * P:(j + 1) * P], wp_t[:],
                                       start=True, stop=True)
                    mm.then_inc(p_ready, 1)
                if stage == NORM2:
                    pe.wait_ge(x2_ready, c + 1)
                    for j, a in enumerate(tiles(c)):
                        mm = pe.transpose(ps[:, 4 + c, j * P:(j + 1) * P], row_of[0][:, a, 0:D], ident[:])
                    mm.then_inc(x2_turned, 1)
                if stage == LOGITS:
                    pe.wait_ge(x2_kept, c + 1)
                    pe.wait_ge(hid_ready, c + 1)
                    for j in range(TC):
                        mm = pe.matmul(ps[:, c, j * EXPERTS:(j + 1) * EXPERTS], turned[:, c, j * P:(j + 1) * P],
                                       router[:], start=True, stop=True)
                    mm.then_inc(logit_ready, 1)
                if stage == ROUTE:
                    pe.wait_ge(hot_ready, s + 1)
                    out = ps[:, 4 + c, 0:TC * EXPERTS]
                    pe.matmul(out, before[:], hot_any[:, chunk(c), :].rearrange("p a e -> p (a e)"),
                              start=True, stop=False)
                    for a in range(TC * c + TC - 1):
                        lo = max(a + 1 - TC * c, 0)
                        mm = pe.matmul(out[:, lo * EXPERTS:], ones[:],
                                       hot_any[:, a, :].unsqueeze(1).broadcast_to([P, TC - lo, EXPERTS]),
                                       start=False, stop=(a == TC * c + TC - 2))
                    mm.then_inc(rank_ready, 1)

            each_stage(run)

            def turn_x(e, u):
                pe.wait_ge(x_loaded[u], (e // 2 + 1) * 16 if isinstance(e, int) else (e - u) * 8 + 16)
                if not (isinstance(e, int) and e < 1):
                    pe.wait_ge(e_kept, e)
                for a in range(CT):
                    mm = pe.transpose(ps[:, a // 4, (a % 4) * P:(a % 4 + 1) * P], x_in[u][:, a, 0:D], ident[:])
                mm.then_inc(e_turned, 1)

            def up(e, u):
                pe.wait_ge(e_kept, e + 1)
                if not (isinstance(e, int) and e < 2):
                    pe.wait_ge(w_loaded[u], e // 2 * 32 if isinstance(e, int) else (e - u) * 16)
                for f in range(FT):
                    if not (isinstance(e, int) and e == 0 and f < 2):
                        pe.wait_ge(h_kept, e * FT + (f - 1))
                    for h in range(2):
                        mm = pe.matmul(ps[:, 2 + 2 * (f % 2) + h, 0:CAP // 2], w1[u][:, f * P:(f + 1) * P],
                                       x_in_t[u][:, h * CAP // 2:(h + 1) * CAP // 2], start=True, stop=True)
                    mm.then_inc(h_full, 1)

            def down(e, u):
                if not (isinstance(e, int) and e < 1):
                    pe.wait_ge(y_kept, e)
                for f in range(FT):
                    pe.wait_ge(h_kept, e * FT + (f + 1))
                    for a in range(CT):
                        mm = pe.matmul(ps[:, 6 + a // 4, (a % 4) * P:(a % 4 + 1) * P],
                                       act_t[u][:, f, a * P:(a + 1) * P], w2[u][:, f, :],
                                       start=(f == 0 and a % 4 == 0), stop=(f == FT - 1 and a in (3, CT - 1)))
                mm.then_inc(y_full, 1)

            pe.wait_ge(slots_ready, S)
            turn_x(0, 0)
            up(0, 0)

            def down_last(e, u):
                pe.wait_ge(h_kept, e * FT + FT)
                pe.wait_ge(y_kept, e)
                for a in range(CT):
                    for f in range(FT):
                        mm = pe.matmul(ps[:, LAST_BANKS[a], 0:P], act_t[u][:, f, a * P:(a + 1) * P], w2[u][:, f, :],
                                       start=(f == 0), stop=(f == FT - 1))
                    mm.then_inc(tile_full, 1)

            def body(e, u):
                if has(e, 1):
                    turn_x(e + 1, 1 - u)
                if isinstance(e, int) and e == E_ - 1:
                    down_last(e, u)
                    return
                down(e, u)
                if has(e, 1):
                    up(e + 1, 1 - u)

            each_expert(pe, body)

        @block.scalar
        def _(act):
            def normalize(i, out, src, c, ready):
                act.wait_ge(scale_ready[i], c + 1)
                for a in tiles(c):
                    last = act.activation(out[:, a, 0:D], src[:, a, :], ACT.Identity,
                                          bias=shift[i][:, a:a + 1], scale=rstd[i][:, a:a + 1])
                last.then_inc(ready, 1)

            def run(stage, c):
                s = c // PER_S
                if stage == TURN_HEADS:
                    act.wait_ge(heads_turned, c + 1)
                    act.copy(turned[:, c, :], ps[:, c, :]).then_inc(heads_kept, 1)
                if stage == NORM1:
                    normalize(1, l1, x1, c, l1_ready)
                if stage == KEEP_L:
                    act.wait_ge(l_turned, c + 1)
                    act.wait_ge(a_ready, c + 1)
                    act.activation(turned[:, c, :], ps[:, c, :], ACT.Identity,
                                   bias=ln[:, 1:2], scale=ln[:, 0:1]).then_inc(l_kept, 1)
                if stage == QKV_KEPT:
                    for h in range(2):
                        act.wait_ge(qkv_ready, 2 * c + h + 1)
                        act.copy(qkv[:, TC * c + 2 * h:TC * c + 2 * h + 2, :].rearrange("p b n -> p (b n)"),
                                 ps[:, 4 + c if h == 0 else c, :]).then_inc(qkv_kept, 1)
                if stage == MIX and s == 1:
                    act.wait_ge(sc_ready, c % PER_S + 1)
                    act.activation(sc_e[c % PER_S][:], sc[c % PER_S][:], ACT.Exp, scale=SCALE).then_inc(sc_exp, 1)
                if stage == PROJECT2:
                    act.wait_ge(att_turned, c + 1)
                    act.copy(turned[:, c, :], ps[:, 4 + c, :]).then_inc(att_kept, 1)
                if stage == NORM2:
                    normalize(2, row_of[0], hid, c, x2_ready)
                if stage == LOGITS:
                    act.wait_ge(x2_turned, c + 1)
                    act.wait_ge(p_ready, c + 1)
                    act.activation(turned[:, c, :], ps[:, 4 + c, :], ACT.Identity,
                                   bias=ln[:, 3:4], scale=ln[:, 2:3]).then_inc(x2_kept, 1)
                if stage == EXP_LOGITS and c % PER_S == PER_S - 1:
                    act.wait_ge(logit_less_max, s + 1)
                    act.activation(lexp[:, TS * s:TS * (s + 1), :], logit[:, TS * s:TS * (s + 1), :],
                                   ACT.Exp).then_inc(exp_ready, 1)

            each_stage(run)

            def body(e, u):
                for f in range(FT):
                    act.wait_ge(h_full, e * FT + (f + 1))
                    if not (isinstance(e, int) and e < 2) and f == 0:
                        act.wait_ge(y_full, e - 1)
                    act.activation(act_t[u][:, f, :].rearrange("p (h n) -> p h n", h=2),
                                   ps[:, 2 + 2 * (f % 2):4 + 2 * (f % 2), 0:CAP // 2],
                                   ACT.Gelu).then_inc(h_kept, 1)

            body(0, 0)
            body(1, 1)
            with act.Fori(0, (E_ - 2) // 2) as turn:
                for u in range(2):
                    body(turn * 2 + (2 + u), u)
            for c in range(CHUNKS):
                normalize(3, base, base, c, normed)

        @block.vector
        def _(dve):
            n = [0]

            def done(ins):
                n[0] += 1
                ins.then_inc(chain, 1)
                dve.wait_ge(chain, n[0])

            def norm_stats(i, src, c):
                for a in tiles(c):
                    last = dve.bn_stats(stats[:, a, :], src[:, a, :])
                done(last)
                for a in tiles(c):
                    last = dve.bn_aggr(mv[i][:, a, :], stats[:, a, :])
                last.then_inc(var_ready[i], 1)

            def scale_and_shift(i, c):
                dve.wait_ge(rstd_ready[i], c + 1)
                dve.scalar_tensor_tensor(out=shift[i][:, chunk(c)], in0=mv[i][:, chunk(c), 0], scalar=-1.0,
                                         in1=rstd[i][:, chunk(c)], op0=ALU.mult,
                                         op1=ALU.mult).then_inc(scale_ready[i], 1)

            def heads(first_tile, lo):
                return qkv[:, first_tile:first_tile + TC, :].rearrange("p b (g c) -> p b g c", g=KV)[:, :, :, lo:lo + DH]

            def query_head(a, pos, r):
                return a[:, :, pos, :].rearrange("p b (g r d) -> p b r g d", g=KV, r=2)[:, :, r]

            def score(c):
                dve.wait_ge(qkv_kept, 2 * c + 2)
                if c % PER_S:
                    dve.wait_ge(sc_ready, c % PER_S)
                for pos in range(2):
                    for r in range(2):
                        last = dve.tensor_tensor(query_head(prod, pos, r), heads(TC * c, DH * r),
                                                 heads(TC * c - TS * (1 - pos), 16), ALU.mult)
                done(last)
                s_ = sc[c % PER_S]
                done(dve.tensor_reduce(s_[:].rearrange("p b t h -> p (b t h)"),
                                       prod[:].rearrange("p b t (h d) -> p (b t h) d", h=H), AX.X, ALU.add))
                done(dve.tensor_tensor(sc_max[:], s_[:, :, 0, :], s_[:, :, 1, :], ALU.max))
                dve.tensor_tensor(s_[:], s_[:], sc_max[:].unsqueeze(2).broadcast_to([P, TC, 2, H]),
                                  ALU.subtract).then_inc(sc_ready, 1)

            def mix_values(c):
                e_ = sc_e[c % PER_S]
                dve.wait_ge(sc_exp, c % PER_S + 1)
                done(dve.tensor_tensor(sc_sum[:], e_[:, :, 0, :], e_[:, :, 1, :], ALU.add))
                done(dve.reciprocal(sc_sum[:], sc_sum[:]))
                done(dve.tensor_tensor(sc_p[:], e_[:], sc_sum[:].unsqueeze(2).broadcast_to([P, TC, 2, H]), ALU.mult))
                for pos in range(2):
                    for r in range(2):
                        p_ = sc_p[:, :, pos, :].rearrange("p b (g r) -> p b r g", g=KV)[:, :, r]
                        last = dve.tensor_tensor(query_head(mix, pos, r), heads(TC * c - TS * (1 - pos), 24),
                                                 p_.unsqueeze(3).broadcast_to([P, TC, KV, DH]), ALU.mult)
                done(last)
                dve.tensor_tensor(att[:, chunk(c), :], mix[:, :, 0, :], mix[:, :, 1, :],
                                  ALU.add).then_inc(att1_ready, 1)
                dve.wait_ge(att1_ready, c % PER_S + 1)

            def less_max(s):
                dve.wait_ge(logit_ready, PER_S * (s + 1))
                mine = slice(TS * s, TS * (s + 1))
                lg = ps[:, PER_S * s:PER_S * (s + 1), 0:TC * EXPERTS].rearrange("p c (a e) -> p c a e", e=EXPERTS)
                mx = lmax[:, mine].rearrange("p (c a) -> p c a", a=TC)
                done(dve.tensor_reduce(mx, lg, AX.X, ALU.max))
                dve.tensor_tensor(logit[:, mine, :].rearrange("p (c a) e -> p c a e", a=TC), lg,
                                  mx.unsqueeze(3).broadcast_to([P, PER_S, TC, EXPERTS]),
                                  ALU.subtract).then_inc(logit_less_max, 1)

            def route(s):
                mine = slice(TS * s, TS * (s + 1))
                bc = lambda a: a[:].unsqueeze(2).broadcast_to([P, TS, EXPERTS])
                e_ = lexp[:, mine, :]
                dve.wait_ge(exp_ready, s + 1)
                done(dve.tensor_reduce(lsum[:], e_, AX.X, ALU.add))
                done(dve.reciprocal(lsum[:], lsum[:]))
                done(dve.tensor_tensor(lprob[:], e_, bc(lsum), ALU.mult))
                order = keep["expert_rank"][:].rearrange("p (a e) -> p a e", e=EXPERTS)
                left = lprob
                for k in range(TOP):
                    done(dve.tensor_reduce(top[k][:], left[:], AX.X, ALU.max))
                    done(dve.tensor_tensor(cand[:], left[:], bc(top[k]), ALU.is_equal))
                    done(dve.tensor_tensor(cand[:], cand[:], order, ALU.mult))
                    done(dve.tensor_reduce(best[:], cand[:], AX.X, ALU.max))
                    done(dve.tensor_tensor(hot[k][:], order, bc(best), ALU.is_equal))
                    if k == 0:
                        done(dve.scalar_tensor_tensor(out=rest[:], in0=hot[0][:], scalar=-2.0, in1=lprob[:],
                                                      op0=ALU.mult, op1=ALU.add))
                        left = rest
                dve.tensor_tensor(hot_any[:, mine, :], hot[0][:], hot[1][:], ALU.add).then_inc(hot_ready, 1)
                done(dve.tensor_tensor(top_sum[:], top[0][:], top[1][:], ALU.add))
                done(dve.reciprocal(top_sum[:], top_sum[:]))
                for k in range(TOP):
                    dve.tensor_tensor(row_of[k][:, mine, WEIGHT], top[k][:], top_sum[:], ALU.mult)
                dve.wait_ge(rank_ready, PER_S * (s + 1))
                rank = ps[:, 4 + PER_S * s:4 + PER_S * (s + 1), 0:TC * EXPERTS]
                done(dve.tensor_tensor(slot_of[:], rank, keep["expert_base"][:].rearrange(
                    "p (c n) -> p c n", c=PER_S), ALU.add))
                done(dve.scalar_tensor_tensor(out=fits[:].rearrange("p (c n) -> p c n", c=PER_S), in0=rank, scalar=float(CAP), in1=slot_of[:],
                                              op0=ALU.is_lt, op1=ALU.mult))
                done(dve.tensor_tensor(picked[:], hots[:], fits[:].unsqueeze(1).broadcast_to(
                    [P, TOP, TS * EXPERTS]), ALU.mult))
                done(dve.tensor_reduce(slot_f[:], picked[:].rearrange("p k (a e) -> p (k a) e", e=EXPERTS),
                                       AX.X, ALU.add))
                dve.tensor_scalar(slot_u[s][:].rearrange("p k a -> p (k a)"), slot_f[:], float(EXPERTS * CAP), None,
                                  ALU.add).then_inc(slots_ready, 1)
                dve.wait_ge(slots_ready, s + 1)

            def run(stage, c):
                s = c // PER_S
                if stage == PROJECT:
                    dve.wait_ge(a_ready, c + 1)
                    dve.tensor_tensor(hid[:, chunk(c), :].rearrange("p a d -> p (a d)"),
                                      x_tok[:, chunk(c), :].rearrange("p a d -> p (a d)"),
                                      ps[:, 4 + c, :], ALU.add).then_inc(a_summed, 1)
                    dve.wait_ge(a_summed, c + 1)
                    norm_stats(0, hid, c)
                if stage == NORM0:
                    dve.wait_ge(rstd_ready[0], c + 1)
                    for a in tiles(c):
                        last = dve.tensor_scalar(x1[:, a, :], hid[:, a, :], mv[0][:, a, 0:1], rstd[0][:, a:a + 1],
                                                 ALU.subtract, ALU.mult)
                    last.then_inc(x1_ready, 1)
                    dve.wait_ge(x1_ready, c + 1)
                    norm_stats(1, x1, c)
                if stage == ROOT1:
                    scale_and_shift(1, c)
                if stage == QKV_KEPT and s == 1:
                    score(c)
                if stage == MIX and s == 1:
                    mix_values(c)
                if stage == PROJECT2:
                    dve.wait_ge(p_ready, c + 1)
                    dve.tensor_tensor(hid[:, chunk(c), :].rearrange("p a d -> p (a d)"),
                                      x1[:, chunk(c), :].rearrange("p a d -> p (a d)"),
                                      ps[:, c, :], ALU.add).then_inc(hid_ready, 1)
                    dve.wait_ge(hid_ready, c + 1)
                    norm_stats(2, hid, c)
                if stage == ROOT2:
                    scale_and_shift(2, c)
                if stage == EXP_LOGITS and c % PER_S == PER_S - 1:
                    less_max(s)
                if stage == ROUTE and c % PER_S == PER_S - 1:
                    route(s)

            each_stage(run)

            def keep_x(e, u):
                dve.wait_ge(e_turned, e + 1)
                if not (isinstance(e, int) and e < 2):
                    dve.wait_ge(h_full, e * FT - FT)
                    dve.wait_ge(y_kept, e - 1)
                dve.tensor_copy(columns[u][:], x_in[u][:, :, TO:XW])
                dve.tensor_scalar(x_in_t[u][:], ps[:, 0:2, :].rearrange("p a n -> p (a n)")[:, 0:CAP],
                                  ln[:, 2:3], ln[:, 3:4], ALU.mult, ALU.add).then_inc(e_kept, 1)

            def keep_y(e, u):
                dve.wait_ge(y_full, e + 1)
                if not (isinstance(e, int) and e < 2):
                    dve.wait_ge(y_sent[u], (e - u) * (16 * CT // 2))
                dve.wait_ge(e_kept, e + 1)
                dve.tensor_copy(y_to[u][:], columns[u][:, :, 0])
                for a in range(CT):
                    last = dve.tensor_scalar(y_out[u][:, a, :], ps[:, 6 + a // 4, (a % 4) * P:(a % 4 + 1) * P],
                                             columns[u][:, a, 1:2], None, ALU.mult)
                last.then_inc(y_kept, 1)

            keep_x(0, 0)
            keep_x(1, 1)
            keep_y(0, 0)
            keep_x(2, 0)
            keep_y(1, 1)
            keep_x(3, 1)
            with dve.Fori(0, (E_ - 4) // 2) as turn:
                for u in range(2):
                    keep_y(turn * 2 + (2 + u), u)
                    keep_x(turn * 2 + (4 + u), u)
            keep_y(E_ - 2, 0)
            e, u = E_ - 1, 1
            dve.wait_ge(y_sent[u], (e - u) * (16 * CT // 2))
            dve.wait_ge(e_kept, e + 1)
            dve.tensor_copy(y_to[u][:], columns[u][:, :, 0])
            for a in range(CT):
                dve.wait_ge(tile_full, a + 1)
                dve.tensor_scalar(y_out[u][:, a, :], ps[:, LAST_BANKS[a], 0:P], columns[u][:, a, 1:2], None,
                                  ALU.mult).then_inc(tile_kept, 1)

            dve.wait_ge(base_ready, CHUNKS)
            for c in range(CHUNKS + 1):
                if c < CHUNKS:
                    dve.wait_ge(fetched[c], 16)
                    for k in range(TOP):
                        done(dve.tensor_tensor(base[:, chunk(c), :], base[:, chunk(c), :],
                                               got[:, chunk(c), k * D:(k + 1) * D], ALU.add))
                    norm_stats(3, base, c)
                if c > 0:
                    scale_and_shift(3, c - 1)


def constants():
    import numpy as np

    def bf16_bits(a):
        return (np.asarray(a, np.float32).view(np.uint32) >> 16).astype(np.uint16)

    n = np.arange(N)
    lo, hi = n % P, n // P * P
    slope = 0.5 ** (np.arange(UNITS) % H)
    block = n // P
    mine = (np.arange(NB)[:, None] == block[None, :]).astype(np.float64)
    sign = np.sign(np.arange(NB)[:, None] - block[None, :])
    alibi_q = np.concatenate([mine, mine, mine * lo])
    alibi_k = slope[:, None, None] * np.concatenate([sign * (hi - P * np.arange(NB)[:, None]), sign * lo, -sign])[None]
    eye = np.eye(P)
    distance = -np.abs(np.arange(P)[:, None] - np.arange(P)[None, :])
    rows, cols = np.arange(P)[:, None], np.arange(P)[None, :]
    experts_ = np.arange(EXPERTS)
    pick = np.zeros((P, 64), np.float32)
    for c in range(4):
        for r in range(DH + 1):
            pick[32 * c + r, 16 * c + r] = 1.0
    return {
        "c_ident": eye.astype(np.float32),
        "c_alibi_q": bf16_bits(alibi_q),
        "c_alibi_k": bf16_bits(alibi_k),
        "c_minus": bf16_bits(-np.ones((PARTS, N))),
        "c_slope_eye": bf16_bits(slope[:, None, None] * eye[None]),
        "c_distance": bf16_bits(distance),
        "c_pick": pick,
        "c_before": bf16_bits(rows < cols),
        "c_experts": np.stack([np.tile(EXPERTS - experts_, TS),
                               np.tile(CAP * experts_ - EXPERTS * CAP, TS)]).astype(np.float32),
        "c_to_row": (TOP * (P * np.arange(NT)[None, None, :] + np.arange(P)[:, None, None])
                     + np.arange(TOP)[None, :, None]).astype(np.float32),
    }


def program(nc, t):
    t["qk_dram"] = nc.dram_tensor("qk_dram", [2, PARTS, S, H * DH, N], BF16).ap()
    t["max_dram"] = nc.dram_tensor("max_dram", [2, PARTS, N], BF16).ap()
    t["xd"] = nc.dram_tensor("xd", [EXPERTS * CAP, XW], F32).ap()
    t["yt"] = nc.dram_tensor("yt", [TOP * NT * P, D], F32).ap()
    with ExitStack() as ctx:
        def sb(name, shape, dt=F32):
            return ctx.enter_context(nc.sbuf_tensor(name, shape, dt))

        keep = {"x_tok": sb("x_tok", [P, NT, D]), "ident": sb("ident", [P, P]),
                "head_out": sb("head_out", [P, NB, UNITS, DH]), **late_buffers(sb)}
        attention_and_prep(nc, t, keep)
        second_half(nc, t, keep)


NAMES = {
    "L0_attn_x": "x", "L0_attn_qkv_w": "qkv_w", "L0_attn_qkv_b": "qkv_b", "L0_attn_out_w": "out_w",
    "L0_attn_out_b": "out_b", "L0_ffn_ln1_weight": "ln1_w", "L0_ffn_ln1_bias": "ln1_b",
    "L0_ffn_ln2_weight": "ln2_w", "L0_ffn_ln2_bias": "ln2_b", "L0_ffn_qkv_weight": "qkv_w2",
    "L0_ffn_proj_weight": "proj_w", "L0_ffn_router_weight": "router", "L0_ffn_moe_w1": "w1", "L0_ffn_moe_w2": "w2",
}


def kernel(**inputs):
    import numpy as _np
    import concourse.bacc as _bacc
    from concourse.bass_utils import run_bass_kernel_spmd as _run

    nc = _bacc.Bacc("TRN2", target_bir_lowering=False, num_devices=1)
    arrays, t = {}, {}
    named = {short: inputs[name] for name, short in NAMES.items()}
    for short, value in {**named, **constants()}.items():
        a = _np.ascontiguousarray(value)
        arrays[f"in_{short}"] = a
        ap = nc.dram_tensor(f"in_{short}", a.shape, mybir.dt.from_np(a.dtype), kind="ExternalInput").ap()
        t[short] = ap.bitcast(BF16) if a.dtype == _np.uint16 else ap
    t["out"] = nc.dram_tensor("out_0", [S, N, D], F32, kind="ExternalOutput").ap()
    program(nc, t)
    return _run(nc, [arrays], core_ids=[0]).results[0]["out_0"]
```
